# Optimizing a Trainium2 kernel written in Bass

```python
import numpy as np
import jax
import jax.numpy as jnp

def _softmax(x, axis=-1):
    return jax.nn.softmax(x, axis=axis)

def _gelu(x):
    return jax.nn.gelu(x, approximate=True)

def _silu(x):
    return jax.nn.silu(x)

def _sigmoid(x):
    return jax.nn.sigmoid(x)

def _layernorm(x, axis=-1, eps=1e-05):
    m = jnp.mean(x, axis=axis, keepdims=True)
    v = jnp.var(x, axis=axis, keepdims=True)
    return (x - m) / jnp.sqrt(v + eps)

def _scatter_add(tgt, idx, src, axis=0):
    return tgt.at[idx].add(src)

def _segment_sum(src, seg, n):
    return jax.ops.segment_sum(src, seg, n)
kernel_name = 'mk_seq_preln_d1_jaxref_r4_f75eec'

def setup_inputs(seed: int=0):
    np.random.seed(seed)
    _w = jnp.asarray

    def _L0_attn_setup():
        import jax, jax.numpy as jnp
        import numpy as np
        D_IN = 256
        D_OUT = 256
        key = jax.random.key(seed)
        kx, kq, kk, kv = jax.random.split(key, 4)
        x = jax.random.normal(kx, (4, 512, D_IN), dtype=jnp.float32)
        s = 1.0 / np.sqrt(D_IN)
        Wq = jax.random.uniform(kq, (D_IN, D_OUT), jnp.float32, -s, s)
        Wk = jax.random.uniform(kk, (D_IN, D_OUT), jnp.float32, -s, s)
        Wv = jax.random.uniform(kv, (D_IN, D_OUT), jnp.float32, -s, s)
        return {'x': x, 'Wq': Wq, 'Wk': Wk, 'Wv': Wv}
    _L0_attn_in = _L0_attn_setup()

    def _L0_ffn_setup():
        import jax, jax.numpy as jnp
        import numpy as np
        B, S, H = (2, 512, 256)
        E_ROUTED = 8
        TOP_K = 2
        I = 512
        key = jax.random.key(seed)
        ks = jax.random.split(key, 9)
        s = 0.02
        return {'x': jax.random.normal(ks[0], (B, S, H), dtype=jnp.float32), 'shared_gate': jax.random.normal(ks[1], (I, H), dtype=jnp.float32) * s, 'shared_up': jax.random.normal(ks[2], (I, H), dtype=jnp.float32) * s, 'shared_down': jax.random.normal(ks[3], (H, I), dtype=jnp.float32) * s, 'gate_w': jax.random.normal(ks[4], (E_ROUTED, H, I), dtype=jnp.float32) * s, 'up_w': jax.random.normal(ks[5], (E_ROUTED, H, I), dtype=jnp.float32) * s, 'down_w': jax.random.normal(ks[6], (E_ROUTED, I, H), dtype=jnp.float32) * s, 'router_w': jax.random.normal(ks[7], (E_ROUTED, H), dtype=jnp.float32) * s, 'routing_bias': jnp.zeros((E_ROUTED,), dtype=jnp.float32)}
    _L0_ffn_in = _L0_ffn_setup()
    _d = {'L0_attn_x': _L0_attn_in['x'], 'L0_attn_Wq': _L0_attn_in['Wq'], 'L0_attn_Wk': _L0_attn_in['Wk'], 'L0_attn_Wv': _L0_attn_in['Wv'], 'L0_ffn_shared_gate': _L0_ffn_in['shared_gate'], 'L0_ffn_shared_up': _L0_ffn_in['shared_up'], 'L0_ffn_shared_down': _L0_ffn_in['shared_down'], 'L0_ffn_gate_w': _L0_ffn_in['gate_w'], 'L0_ffn_up_w': _L0_ffn_in['up_w'], 'L0_ffn_down_w': _L0_ffn_in['down_w'], 'L0_ffn_router_w': _L0_ffn_in['router_w'], 'L0_ffn_routing_bias': _L0_ffn_in['routing_bias']}
    _x0 = _d['L0_attn_x']
    _d['L0_attn_x'] = jax.random.normal(jax.random.fold_in(jax.random.key(seed), 1), (8, 512, 256), dtype=_x0.dtype)
    del _x0
    return _d

def reference(L0_attn_x, L0_attn_Wq, L0_attn_Wk, L0_attn_Wv, L0_ffn_shared_gate, L0_ffn_shared_up, L0_ffn_shared_down, L0_ffn_gate_w, L0_ffn_up_w, L0_ffn_down_w, L0_ffn_router_w, L0_ffn_routing_bias):

    def _L0_attn_ref(x, Wq, Wk, Wv):
        import jax, jax.numpy as jnp
        import numpy as np
        D_IN = 256
        D_OUT = 256
        n = x.shape[1]
        q = jnp.einsum('bnd,de->bne', x, Wq)
        k = jnp.einsum('bnd,de->bne', x, Wk)
        v = jnp.einsum('bnd,de->bne', x, Wv)
        scores = jnp.einsum('bqe,bke->bqk', q, k)
        causal = jnp.tril(jnp.ones((n, n), dtype=bool))
        scores = jnp.where(causal, scores, -jnp.inf)
        attn = jax.nn.softmax(scores / jnp.sqrt(jnp.float32(k.shape[-1])), axis=-1)
        return jnp.einsum('bqk,bke->bqe', attn, v)

    def _L0_ffn_ref(x, shared_gate, shared_up, shared_down, gate_w, up_w, down_w, router_w, routing_bias):
        import jax, jax.numpy as jnp
        import numpy as np
        B, S, H = (2, 512, 256)
        E_ROUTED = 8
        TOP_K = 2
        I = 512
        b, s, h = x.shape
        shared = jnp.einsum('bsi,hi->bsh', jax.nn.silu(jnp.einsum('bsh,ih->bsi', x, shared_gate)) * jnp.einsum('bsh,ih->bsi', x, shared_up), shared_down)
        logits = jnp.einsum('bsh,eh->bse', x, router_w) + routing_bias
        probs = jax.nn.sigmoid(logits)
        scores, indices = jax.lax.top_k(probs, TOP_K)
        scores = scores / jnp.sum(scores, axis=-1, keepdims=True)
        t = b * s
        xf = x.reshape(t, h)
        idx = indices.reshape(t, TOP_K)
        sc = scores.reshape(t, TOP_K)
        w = jnp.zeros((t, E_ROUTED), dtype=x.dtype)
        w = w.at[jnp.arange(t)[:, None], idx].add(sc)
        g = jax.nn.silu(jnp.einsum('th,ehi->tei', xf, gate_w))
        u = jnp.einsum('th,ehi->tei', xf, up_w)
        combined = jnp.einsum('tei,eih,te->th', g * u, down_w, w)
        return shared + combined.reshape(b, s, h)
    x = L0_attn_x
    x = x + _L0_attn_ref(_layernorm(x, axis=-1), L0_attn_Wq, L0_attn_Wk, L0_attn_Wv)
    x = x + _L0_ffn_ref(_layernorm(x, axis=-1), L0_ffn_shared_gate, L0_ffn_shared_up, L0_ffn_shared_down, L0_ffn_gate_w, L0_ffn_up_w, L0_ffn_down_w, L0_ffn_router_w, L0_ffn_routing_bias)
    return x

_drawn_inputs = setup_inputs


def setup_inputs(seed=0):
    import zlib

    import numpy as np

    out = dict(_drawn_inputs(seed))
    spreads = {'L0_ffn_routing_bias': (0.0, 0.8)}
    factors = {'L0_ffn_gate_w': 3.398,
     'L0_ffn_up_w': 3.355,
     'L0_ffn_down_w': 3.355,
     'L0_ffn_router_w': 3.923,
     'L0_ffn_shared_gate': 2.858,
     'L0_ffn_shared_up': 2.692,
     'L0_ffn_shared_down': 2.703}
    for name, (base, spread) in spreads.items():
        noise = np.random.default_rng([zlib.crc32(name.encode()), seed]).standard_normal(out[name].shape)
        drawn = base * np.exp(spread * noise) if base else spread * noise
        out[name] = jnp.asarray(drawn.astype(out[name].dtype))
    for name, factor in factors.items():
        out[name] = (out[name] * factor).astype(out[name].dtype)
    return out
```

```python
from contextlib import ExitStack

import concourse.bass as bass
from concourse import mybir

F32 = mybir.dt.float32
F16 = mybir.dt.float16
BF16 = mybir.dt.bfloat16
I32 = mybir.dt.int32
ALU = mybir.AluOpType
ACT = mybir.ActivationFunctionType
X = mybir.AxisListType.X
ds = bass.ds

P = 128
B, S, D = 8, 512, 256
T = B * S
E, TOPK, I = 8, 2, 512
NB = S // P
KD = D // P
KI = I // P
TT = 256
TILES = (TOPK * T - E) // TT + E
EPS = 1e-5
WS = 16.0
NEG = -1e30

MAT = KD * I
WJ = 3 * MAT
CH = WJ // 4
CHUNKS = 4

REG = T + TT
SPARE = E * REG
LIN = SPARE + TT
ROWS = LIN + T
RW = 2 * D + 2
YROWS = TOPK * T + (E + 1) * TT

EARLY = 4
LATE = 5
N0, N1, NF = EARLY, EARLY + TILES, EARLY + TILES + LATE
INLINE = B - 1


def wait(eng, sem, value):
    if isinstance(value, int) and value <= 0:
        return
    eng.wait_ge(sem, value)


def gate(eng, sem, value, passed):
    if isinstance(value, int) and value <= 0:
        return
    eng.wait_ge(sem, value)
    eng.sem_inc(passed, 1)


class Chain:

    def __init__(self, eng, sem, per, run):
        self.eng, self.sem, self.per, self.run, self.k = eng, sem, per, run, 0

    def then(self, ins):
        ins.then_inc(self.sem, 1)
        self.k += 1
        assert self.k <= self.per
        return ins

    def last(self):
        self.eng.wait_ge(self.sem, self.run * self.per + self.k)


def build(nc, x, wq_t, wk_t, wv, w_all, router, bias, out):
    with ExitStack() as ctx:
        ctx.enter_context(nc.allow_low_precision(reason="sums of whole numbers below 2^24, written as int32"))

        def sb(name, width, dt):
            return ctx.enter_context(nc.sbuf_tensor(name, [P, width], dt))

        def sem(name):
            return ctx.enter_context(nc.semaphore(name))

        rows = nc.dram_tensor("rows", [ROWS, RW], F16, kind="Internal").ap()
        ytok = nc.dram_tensor("ytok", [YROWS, D], F32, kind="Internal").ap()

        w = sb("w", (E + 1) * 2 * WJ, F16)
        x1 = sb("x1", B * NB * D, F32)
        wm = sb("wm", 2 * KD * D, F16)
        wvs = sb("wvs", 2 * KD * D, F16)
        rw = sb("rw", 2 * KD * E, F16)
        biases = sb("biases", NB * E, F32)
        wk = sb("wk", TOPK * B * NB, F32)
        arena = sb("arena", 4096, F32)
        xn32 = arena[:, 0:1024]
        xnrow = arena[:, 1024:2048].bitcast(F16)
        tt = arena[:, 2048:3072].bitcast(F16)
        v = arena[:, 3072:4096].bitcast(F16)
        xnt = sb("xnt", 2 * KD * S, F16)
        p32 = sb("p32", 2 * S, F32)
        phl = sb("phl", 2 * 2 * S, F16)
        ptr = sb("ptr", 2 * P * (NB * (NB + 1) // 2), F16)
        xrow = [sb(f"xrow{k}", NB * RW, F16) for k in range(TOPK)]
        xn2t = sb("xn2t", 2 * KD * S, F16)
        th = sb("th", 2 * 2 * TT, F32)
        h = sb("h", 2 * KI * TT, F16)
        wst = sb("wst", 2 * CH, F32)
        ident = sb("ident", P, BF16)
        maskb = sb("maskb", P, BF16)
        tri = sb("tri", P, F16)
        ones = sb("ones", P, F16)
        halves = sb("halves", NB, F32)
        rev = sb("rev", NB * E, F32)
        base = sb("base", NB * E, F32)
        tokidx = sb("tokidx", B * TOPK * NB, I32)
        padidx = sb("padidx", (E + 1) * (TT // P), I32)
        stats = sb("stats", NB * 6, F32)
        mv = sb("mv", NB * 2, F32)
        ve = sb("ve", NB, F32)
        rstd = sb("rstd", NB, F32)
        mx = sb("mx", NB, F32)
        nm = sb("nm", NB, F32)
        sums = sb("sums", NB, F32)
        s16 = sb("s16", NB, F32)
        rs = sb("rs", NB, F32)
        z = sb("z", NB * E, F32)
        ez = sb("ez", NB * E, F32)
        pr = sb("pr", NB * E, F32)
        pr2 = sb("pr2", NB * E, F32)
        eq = sb("eq", NB * E, F32)
        one_hot = [sb(f"one_hot{k}", NB * E, F32) for k in range(TOPK)]
        m12 = [sb(f"m{k}", NB, F32) for k in range(TOPK)]
        rk = sb("rk", NB, F32)
        den = sb("den", NB, F32)
        rden = sb("rden", NB, F32)
        mask = sb("mask", NB * E, F16)
        msum = sb("msum", E, F32)
        cum = sb("cum", E, F32)
        cumh = sb("cumh", E, F16)
        pos = sb("pos", NB * E, F32)
        pm = sb("pm", NB * E, F32)
        sidx = sb("sidx", TOPK * NB, I32)
        yidx = sb("yidx", 2 * 2, I32)
        start_tab = sb("start_tab", NF, I32)
        w_tab = sb("w_tab", NF, I32)
        ti = sb("ti", E, I32)
        tneg = sb("tneg", TILES, F32)
        erow = sb("erow", 2 * E, F32)
        xt = xnt
        ysb = p32
        tabs = phl[:, :].bitcast(F32)
        tio, oh, ot = (tabs[:, i * TILES * E:(i + 1) * TILES * E] for i in range(3))
        tf = tabs[:, 3 * TILES * E:3 * TILES * E + 7 * E]
        yin = [arena[:, 2048 * s:2048 * (s + 1)] for s in range(2)]

        bank = [ctx.enter_context(nc.psum_tensor(f"bank{i}", [P, 512], F32)) for i in range(8)]
        G, U, Y = [bank[0], bank[2]], [bank[1], bank[3]], bank[4]
        PT0, PT1, PT2 = bank[5], bank[6], bank[7]

        c_rdy = sem("c_rdy")
        c_dve = sem("c_dve")
        small_in = sem("small_in")
        x_first, x_rest = sem("x_first"), sem("x_rest")
        qk_in = sem("qk_in")
        prep_mm = sem("prep_mm")
        prep_hi = sem("prep_hi")
        prep_lo = sem("prep_lo")
        w_in = [sem("w_in0"), sem("w_in1")]
        w_hi = sem("w_hi")
        w_lo = sem("w_lo")
        pad_in = sem("pad_in")
        ln_dve = sem("ln_dve")
        ln_rstd = sem("ln_rstd")
        ln_hi = sem("ln_hi")
        xn_lo = sem("xn_lo")
        xn2_lo = sem("xn2_lo")
        xn2_dup = sem("xn2_dup")
        idx_put = sem("idx_put")
        xnt_in = sem("xnt_in")
        xn2t_in = sem("xn2t_in")
        lin_out = sem("lin_out")
        t_mm, t_hi, t_lo = sem("t_mm"), sem("t_hi"), sem("t_lo")
        v_mm, v_hi, v_lo = sem("v_mm"), sem("v_hi"), sem("v_lo")
        s_mm = sem("s_mm")
        s_max, s_nm = sem("s_max"), sem("s_nm")
        s_exp, p_hi, p_lo = sem("s_exp"), sem("p_hi"), sem("p_lo")
        pt_in = [sem(f"pt_in{q}") for q in range(NB)]
        pv_mm = sem("pv_mm")
        sum_dve = sem("sum_dve")
        x1_put = sem("x1_put")
        lg_mm, lg_read = sem("lg_mm"), sem("lg_read")
        r_exp, r_dve = sem("r_exp"), sem("r_dve")
        px_mm, px_dve = sem("px_mm"), sem("px_dve")
        sidx_rdy = sem("sidx_rdy")
        scat = sem("scat")
        cnt_mm = sem("cnt_mm")
        tab = sem("tab")
        tio_rdy = sem("tio_rdy")
        gu_mm = sem("gu_mm")
        f_tanh, f_sg, f_h, f_hi, f_lo = sem("f_tanh"), sem("f_sg"), sem("f_h"), sem("f_hi"), sem("f_lo")
        dn_mm = sem("dn_mm")
        y_read = sem("y_read")
        xt_in = [sem("xt_in0"), sem("xt_in1")]
        yi_in = [sem("yi_in0"), sem("yi_in1")]
        y_out = sem("y_out")
        yin_in = [sem("yin_in0"), sem("yin_in1")]
        c_k0, c_put = sem("c_k0"), sem("c_put")
        out_done = sem("out_done")
        sp_past, pool_past, dve_past = sem("sp_past"), sem("pool_past"), sem("dve_past")

        R_STEPS = 19
        LN_STEPS = 10
        T_STEPS = 20

        def blk(t3):
            return t3.rearrange("p (n d) -> p n d", n=NB)

        def w_ap(j, part, off, n):
            return w[:, ds(j * (2 * WJ) + (part * WJ + off), n)]

        PASSES = ((0, 0), (0, 1), (1, 0))

        block = ctx.enter_context(nc.Block())

        @block.sync
        def _(sp):
            sp.dma_start(x1[:, 0:NB * D].rearrange("p (n d) -> p n d", n=NB),
                         x[0:S, :].rearrange("(n p) d -> p n d", p=P)).then_inc(x_first, 16)
            sp.dma_start(v[:, 0:1024].bitcast(F32).rearrange("p (k d) -> p k d", k=KD),
                         wq_t.rearrange("(k p) d -> p k d", p=P)).then_inc(qk_in, 16)
            sp.dma_start(v[:, 1024:2048].bitcast(F32).rearrange("p (k d) -> p k d", k=KD),
                         wk_t.rearrange("(k p) d -> p k d", p=P)).then_inc(qk_in, 16)
            sp.dma_start(tt[:, 0:1024].bitcast(F32).rearrange("p (k d) -> p k d", k=KD),
                         wv.rearrange("(k p) d -> p k d", p=P)).then_inc(qk_in, 16)
            sp.dma_start(tt[:, 1024:1024 + 2 * KD * E].bitcast(F32).rearrange("p (k d) -> p k d", k=KD),
                         router.rearrange("(k p) d -> p k d", p=P)).then_inc(small_in, 16)
            sp.dma_start(biases[:, 0:E], bias.partition_broadcast(P)).then_inc(small_in, 16)

            def w_load(chunk, slot):
                gate(sp, w_lo, chunk - 1, sp_past)
                sp.dma_start(wst[:, slot * CH:(slot + 1) * CH],
                             w_all[:, ds(chunk * CH, CH)]).then_inc(w_in[slot], 16)

            w_load(0, 0)
            w_load(1, 1)
            for b in range(1, B):
                sp.dma_start(blk(x1[:, b * NB * D:(b + 1) * NB * D]),
                             x[b * S:(b + 1) * S, :].rearrange("(n p) d -> p n d", p=P)).then_inc(x_rest, 16)

            def xn_transpose(b):
                gate(sp, s_mm, NB * b, sp_past)
                gate(sp, xn_lo, b + 1, sp_past)
                sp.dma_start_transpose(xnt[:, :].rearrange("p (n r) -> p n r", r=P),
                                       xnrow).then_inc(xnt_in, 16)

            xn_transpose(0)
            for chunk in (2, 3):
                w_load(chunk, chunk % 2)
            sp.wait_ge(c_dve, 1)
            sp.wait_ge(c_rdy, 1)
            for e in range(E + 1):
                pad = rows[e * REG:e * REG + TT, :].rearrange("(a p) c -> p a c", p=P)
                sp.dma_start(pad[:, :, 0:2 * D],
                             xrow[0][:, 0:4 * D].rearrange("p (a c) -> p a c", a=2)).then_inc(pad_in, 16)
                sp.dma_start(pad[:, :, 2 * D:RW],
                             padidx[:, 2 * e:2 * e + 2].bitcast(F16).rearrange("p (a c) -> p a c", a=2)
                             ).then_inc(pad_in, 16)

            def batch(b, first=False, final=False):
                for i in range(2):
                    w_load(b * CHUNKS + CHUNKS + i, i)
                off = 0
                for q in range(NB):
                    n = (q + 1) * P
                    gate(sp, pv_mm, 2 * b, sp_past)
                    gate(sp, p_lo, NB * b + q + 1, sp_past)
                    sp.dma_start_transpose(
                        ptr[:, off:off + 2 * n].rearrange("p (n r) -> p n r", r=P),
                        phl[:, (q % 2) * 2 * S:(q % 2) * 2 * S + 2 * n]).then_inc(pt_in[q], 16)
                    off += 2 * n
                for i in range(2, CHUNKS):
                    w_load(b * CHUNKS + CHUNKS + i, i % 2)
                if not final:
                    xn_transpose(b + 1)
                gate(sp, gu_mm, 2 * b, sp_past)
                gate(sp, xn2_lo, b + 1, sp_past)
                for i in range(NB):
                    sp.dma_start_transpose(
                        xn2t[:, i * 4 * P:(i + 1) * 4 * P].rearrange("p (n r) -> p n r", r=P),
                        xrow[0][:, i * RW:i * RW + 2 * D]).then_inc(xn2t_in, 16)
                gate(sp, idx_put, TOPK * b + 1, sp_past)
                sp.dma_start(rows[ds(LIN + b * S, S), :].rearrange("(n p) c -> p n c", p=P),
                             xrow[0][:, :].rearrange("p (n c) -> p n c", n=NB)).then_inc(lin_out, 16)

            batch(0, first=True)
            with sp.Fori(1, B - 1) as b:
                batch(b)
            batch(B - 1, final=True)

            def load_tile(n, slot):
                row = sp.value_load(start_tab[0:1, ds(n, 1)], min_val=0, max_val=ROWS - TT)
                gate(sp, gu_mm, n * 2 + (2 * INLINE - 2), sp_past)
                sp.dma_start_transpose(
                    xt[:, slot * 4 * TT:(slot + 1) * 4 * TT].rearrange("p (c r) -> p c r", r=TT),
                    rows[ds(row, TT), 0:2 * D]).then_inc(xt_in[slot], 16)
                return row

            def load_yidx(n, row, slot):
                gate(sp, y_out, n * 32 - (N0 + 1) * 32, sp_past)
                sp.dma_start(yidx[:, 2 * slot:2 * slot + 2].bitcast(F16).rearrange("p (a c) -> p a c", a=2),
                             rows[ds(row, TT), 2 * D:RW].rearrange("(a p) c -> p a c", p=P)
                             ).then_inc(yi_in[slot], 16)

            sp.wait_ge(s_mm, NB * B)
            sp.wait_ge(lin_out, 16 * B)
            load_tile(0, 0)
            load_tile(1, 1)
            with sp.Fori(2, N0 - 1, 2) as n:
                for s in range(2):
                    load_tile(n + s, s)
            sp.wait_ge(tab, T_STEPS)
            sp.wait_ge(scat, B * TOPK * NB * 16)
            sp.wait_ge(pad_in, 2 * (E + 1) * 16)

            def expert_tile(n, slot, peeled=False):
                row = load_tile(n, slot)
                if peeled:
                    sp.dma_start(yidx[:, 2 * slot:2 * slot + 2].bitcast(F16).rearrange("p (a c) -> p a c", a=2),
                                 rows[ds(row, TT), 2 * D:RW].rearrange("(a p) c -> p a c", p=P)
                                 ).then_inc(yi_in[slot], 16)
                else:
                    load_yidx(n, row, slot)

            expert_tile(N0, 0, True)
            expert_tile(N0 + 1, 1, True)
            with sp.Fori(N0 + 2, N1 - 2, 2) as n:
                for s in range(2):
                    expert_tile(n + s, s)
            expert_tile(N1 - 1, (N1 - 1) % 2)
            load_tile(N1, N1 % 2)
            with sp.Fori(N1 + 1, NF - 1, 2) as n:
                for s in range(2):
                    load_tile(n + s, (N1 + 1 + s) % 2)

            def y_load(b, slot):
                sp.dma_start(yin[slot].rearrange("p (n c) -> p n c", n=NB),
                             ytok[ds(b * (S * TOPK), S * TOPK), :].rearrange(
                                 "(n p k) d -> p n (k d)", n=NB, k=TOPK)).then_inc(yin_in[slot], 16)

            sp.wait_ge(y_out, TILES * 32)
            y_load(0, 0)
            y_load(1, 1)
            with sp.Fori(2, B - 1, 2) as b:
                for s in range(2):
                    gate(sp, c_put, (b + s) * NB - NB, sp_past)
                    y_load(b + s, s)
            sp.wait_ge(out_done, 16 * B)

        @block.gpsimd
        def _(pool):
            cc = nc.gpsimd
            steps = [0]

            def const(ins):
                ins.then_inc(c_rdy, 1)
                steps[0] += 1

            def const_wait():
                pool.wait_ge(c_rdy, steps[0])

            const(cc.iota(padidx[:, :].rearrange("p (e a) -> p e a", a=2), pattern=[[TT, E + 1], [P, 2]],
                          base=TOPK * T, channel_multiplier=1))
            const(cc.iota(tokidx[:, :].rearrange("p (b k n) -> p b k n", b=B, k=TOPK),
                          pattern=[[TOPK * S, B], [1, TOPK], [TOPK * P, NB]], base=0, channel_multiplier=TOPK))
            const(cc.memset(ident[:, :], 0.0))
            const(cc.memset(maskb[:, :], 0.0))
            const(cc.memset(tri[:, :], 1.0))
            const(cc.memset(ones[:, :], 1.0))
            const(cc.memset(halves[:, :], -0.5))
            const_wait()
            const(cc.affine_select(out=ident[:, :], in_=ident[:, :], compare_op=ALU.not_equal, fill=1.0,
                                   base=0, pattern=[[-1, P]], channel_multiplier=1))
            const(cc.affine_select(out=maskb[:, :], in_=maskb[:, :], compare_op=ALU.is_ge, fill=NEG,
                                   base=0, pattern=[[-1, P]], channel_multiplier=1))
            const(cc.affine_select(out=tri[:, :], in_=tri[:, :], compare_op=ALU.is_gt, fill=0.0,
                                   base=0, pattern=[[1, P]], channel_multiplier=-1))
            imp = dict(allow_small_or_imprecise_dtypes=True)
            const(cc.iota(rev[:, :].rearrange("p (n e) -> p n e", n=NB), pattern=[[0, NB], [-1, E]],
                          base=E, channel_multiplier=0, **imp))
            const(cc.iota(base[:, :].rearrange("p (n e) -> p n e", n=NB), pattern=[[0, NB], [REG, E]],
                          base=TT, channel_multiplier=0, **imp))
            const(cc.iota(tneg[:, :], pattern=[[-TT, TILES]], base=-SPARE, channel_multiplier=0, **imp))
            const(cc.iota(erow[:, 0:E], pattern=[[REG, E]], base=0, channel_multiplier=0, **imp))
            const(cc.iota(erow[:, E:2 * E], pattern=[[1, E]], base=1, channel_multiplier=0, **imp))
            const(cc.iota(start_tab[:, 0:N0], pattern=[[S, EARLY]], base=LIN + TT, channel_multiplier=0))
            const(cc.iota(start_tab[:, N1:N1 + LATE - 1], pattern=[[S, LATE - 1]],
                          base=LIN + TT + EARLY * S, channel_multiplier=0))
            const(cc.iota(start_tab[:, NF - 1:NF], pattern=[[0, 1]], base=LIN + (B - 1) * S,
                          channel_multiplier=0))
            const(cc.iota(w_tab[:, 0:N0], pattern=[[0, N0]], base=0, channel_multiplier=0))
            const(cc.iota(w_tab[:, N1:NF], pattern=[[0, LATE]], base=0, channel_multiplier=0))
            const_wait()

            def rstd_of(run):
                pool.wait_ge(ln_dve, run * LN_STEPS + 6)
                cc.tensor_tensor(rstd[:, :], ve[:, :], halves[:, :], ALU.pow).then_inc(ln_rstd, 1)

            def xn_low(b, run):
                wait(pool, xnt_in, 16 * b)
                pool.wait_ge(ln_hi, run + 1)
                cc.tensor_tensor(xnrow.rearrange("p (n c) -> p n c", n=NB)[:, :, D:2 * D], blk(xn32),
                                 xnrow.rearrange("p (n c) -> p n c", n=NB)[:, :, 0:D],
                                 ALU.subtract).then_inc(xn_lo, 1)

            def put_idx(b):
                wait(pool, scat, 16 * TOPK * NB * b)
                wait(pool, lin_out, 16 * b)
                pool.wait_ge(pad_in, 2 * (E + 1) * 16)
                for k in range(TOPK):
                    cc.tensor_copy(
                        xrow[k][:, :].bitcast(I32).rearrange("p (n c) -> p n c", n=NB)[:, :, D],
                        tokidx[:, ds(b * (TOPK * NB) + k * NB, NB)]).then_inc(idx_put, 1)

            def scatter(b):
                gate(pool, sidx_rdy, b * 2 + 2, pool_past)
                gate(pool, xn2_dup, b + 1, pool_past)
                gate(pool, idx_put, TOPK * b + TOPK, pool_past)
                for n in range(NB):
                    for k in range(TOPK):
                        cc.indirect_dma_start(
                            rows[0:SPARE, :], bass.IndirectOffsetOnAxis(ap=sidx[:, k * NB + n:k * NB + n + 1], axis=0),
                            xrow[k][:, n * RW:(n + 1) * RW], None).then_inc(scat, 16)

            rstd_of(0)
            xn_low(0, 0)

            def batch(b, first=False, final=False):
                if not final:
                    rstd_of(2 * b + 1)
                    xn_low(b + 1, 2 * b + 1)
                if not first:
                    scatter(b - 1)
                rstd_of(2 * b + 2 if not final else 2 * b + 1)
                put_idx(b)

            batch(0, first=True)
            with pool.Fori(1, B - 1) as b:
                batch(b)
            batch(B - 1, final=True)
            for q in range(2, NB):
                pool.wait_ge(pt_in[q], 16 * B)
            cc.iota(tio.rearrange("p (t e) -> p t e", t=TILES), pattern=[[1, TILES], [0, E]],
                    base=0, channel_multiplier=0, **imp).then_inc(tio_rdy, 1)
            scatter(B - 1)

            def y_scatter(n, slot):
                cnt = (n - N0 - slot) * 8 + 16 if not isinstance(n, int) else ((n - N0) // 2 + 1) * 16
                gate(pool, y_read, n + (INLINE + 1), pool_past)
                gate(pool, yi_in[slot], cnt, pool_past)
                for a in range(2):
                    cc.indirect_dma_start(
                        ytok, bass.IndirectOffsetOnAxis(ap=yidx[:, 2 * slot + a:2 * slot + a + 1], axis=0),
                        ysb[:, a * D:(a + 1) * D], None).then_inc(y_out, 16)

            with pool.Fori(N0, N1 - 2, 2) as n:
                for s in range(2):
                    y_scatter(n + s, s)
            y_scatter(N1 - 1, (N1 - 1) % 2)

        @block.scalar
        def _(act):
            a = nc.scalar

            def copy(o, i, scale=1.0):
                return a.activation(o, i, ACT.Copy, scale=scale)

            act.wait_ge(qk_in, 48)
            act.wait_ge(small_in, 32)
            copy(wvs[:, 0:KD * D], tt[:, 0:1024].bitcast(F32), WS).then_inc(prep_hi, 1)
            copy(rw[:, 0:KD * E], tt[:, 1024:1024 + 2 * KD * E].bitcast(F32), WS).then_inc(prep_hi, 1)
            act.wait_ge(prep_mm, 1)
            copy(wm[:, 0:KD * D], PT0[:, :], WS).then_inc(prep_hi, 1)

            def w_split(chunk, slot, cnt, j, c):
                act.wait_ge(w_in[slot], cnt)
                copy(w[:, ds(j * (2 * WJ) + c * CH, CH)], wst[:, slot * CH:(slot + 1) * CH], WS).then_inc(w_hi, 1)

            for c in range(2):
                w_split(c, c, 16, 0, c)

            def ln_high(dst, run, free=()):
                act.wait_ge(ln_dve, run * LN_STEPS + LN_STEPS)
                for s_, v_ in free:
                    wait(act, s_, v_)
                copy(dst, blk(xn32)).then_inc(ln_hi, 1)

            def xn_high(b, run):
                ln_high(xnrow.rearrange("p (n c) -> p n c", n=NB)[:, :, 0:D], run, [(xnt_in, 16 * b)])

            xn_high(0, 0)
            for c in range(2, CHUNKS):
                w_split(c, c % 2, 32, 0, c)

            def ffn_half(t, half, inline=False):
                act.wait_ge(gu_mm, t * 2 + half + 1)
                if not inline:
                    act.wait_ge(f_lo, t * 2 - 2 + half + 1)
                a.activation(th[:, half * 512:(half + 1) * 512], G[half][:, :], ACT.Tanh,
                             scale=0.5 / WS).then_inc(f_tanh, 1)
                act.wait_ge(f_h, t * 2 + half + 1)
                if not inline:
                    act.wait_ge(dn_mm, t * 2 - 2 + half + 1)
                copy(h[:, half * 512:(half + 1) * 512], th[:, half * 512:(half + 1) * 512]).then_inc(f_hi, 1)

            def batch(b, first=False, final=False):
                for m in range(KD):
                    act.wait_ge(t_mm, KD * b + m + 1)
                    if first:
                        act.wait_ge(prep_lo, 3)
                    wait(act, s_mm, NB * b)
                    copy(tt[:, m * S:(m + 1) * S], (PT0, PT1)[m][:, :]).then_inc(t_hi, 1)
                for m in range(2):
                    act.wait_ge(v_mm, 2 * b + m + 1)
                    wait(act, pv_mm, 2 * b)
                    copy(v[:, m * S:(m + 1) * S], (PT2, PT0)[m][:, :]).then_inc(v_hi, 1)
                if not final:
                    xn_high(b + 1, 2 * b + 1)
                if not first:
                    act.wait_ge(lg_read, b)
                    a.activation(ez[:, :], z[:, :], ACT.Exp, scale=-1.0).then_inc(r_exp, 1)
                for c in range(2):
                    w_split(None, c, 32 * b + 48, b + 1, c)
                for q in range(NB):
                    n = (q + 1) * P
                    sbank = (PT2, PT0, PT1, PT2)[q]
                    act.wait_ge(s_nm, NB * b + q + 1)
                    if q < 2:
                        wait(act, p_lo, NB * b - 2 + q + 1)
                    else:
                        act.wait_ge(p_lo, NB * b + q - 1)
                    if q == 0:
                        wait(act, x1_put, NB * b)
                    a.activation(p32[:, (q % 2) * S:(q % 2) * S + n], sbank[:, 0:n], ACT.Exp,
                                 bias=nm[:, q:q + 1], scale=1.0 / (16.0 * WS),
                                 accum_out=sums[:, q:q + 1]).then_inc(s_exp, 1)
                    act.wait_ge(s_exp, NB * b + q + 1)
                    if q < 2:
                        wait(act, pt_in[q + 2], 16 * b)
                    else:
                        act.wait_ge(pt_in[q - 2], 16 * b + 16)
                    copy(phl[:, (q % 2) * 2 * S:(q % 2) * 2 * S + n],
                         p32[:, (q % 2) * S:(q % 2) * S + n]).then_inc(p_hi, 1)
                if not first:
                    for half in range(2):
                        ffn_half(b - 1, half, inline=True)
                for c in range(2, CHUNKS):
                    w_split(None, c % 2, 32 * b + 64, b + 1, c)
                run = 2 * b + 2 if not final else 2 * b + 1
                ln_high(xrow[0][:, :].rearrange("p (n c) -> p n c", n=NB)[:, :, 0:D], run,
                        [(xn2t_in, 64 * b), (scat, 16 * TOPK * NB * b), (lin_out, 16 * b)]
                        + ([(pad_in, 2 * (E + 1) * 16)] if first else []))

            batch(0, first=True)
            with act.Fori(1, B - 1) as b:
                batch(b)
            batch(B - 1, final=True)
            act.wait_ge(lg_read, B)
            a.activation(ez[:, :], z[:, :], ACT.Exp, scale=-1.0).then_inc(r_exp, 1)

            def y_copy(n):
                act.wait_ge(dn_mm, n * 2 + 2 * INLINE + 2)
                wait(act, y_out, n * 32 - N0 * 32)
                copy(ysb[:, 0:2 * D], Y[:, :]).then_inc(y_read, 1)

            def tile(n, expert_before):
                ffn_half(n + INLINE, 0)
                if expert_before:
                    y_copy(n - 1)
                ffn_half(n + INLINE, 1)

            tile(0, False)
            with act.Fori(1, N0 + 1) as n:
                tile(n, False)
            with act.Fori(N0 + 1, N1 + 1) as n:
                tile(n, True)
            with act.Fori(N1 + 1, NF) as n:
                tile(n, False)
            with act.Fori(0, B) as b:
                act.wait_ge(c_put, b * NB + NB)
                act.dma_start(out[ds(b * S, S), :].rearrange("(n p) d -> p n d", p=P),
                              blk(x1[:, ds(b * (NB * D), NB * D)])).then_inc(out_done, 16)

        @block.vector
        def _(dve):
            d = nc.vector
            d.memset(xrow[0][:, 0:4 * D], 0.0).then_inc(c_dve, 1)
            d.memset(cum[:, :], 0.0).then_inc(c_dve, 1)
            d.memset(cumh[:, :], 0.0).then_inc(c_dve, 1)

            def low(o, full, hi, scale=None):
                if scale is None:
                    return d.tensor_tensor(o, full, hi, ALU.subtract)
                return d.scalar_tensor_tensor(out=o, in0=full, scalar=scale, in1=hi, op0=ALU.mult, op1=ALU.subtract)

            def w_low(g, slot, j, c):
                wait(dve, w_hi, g + 1)
                low(w[:, ds(j * (2 * WJ) + (WJ + c * CH), CH)], wst[:, slot * CH:(slot + 1) * CH],
                    w[:, ds(j * (2 * WJ) + c * CH, CH)], WS).then_inc(w_lo, 1)

            def normalise(src, run):
                c = Chain(dve, ln_dve, LN_STEPS, run)
                for i in range(NB):
                    ins = d.bn_stats(stats[:, 6 * i:6 * i + 6], src(i))
                c.then(ins)
                gate(dve, ln_dve, run * LN_STEPS + 1, dve_past)
                for i in range(NB):
                    c.then(d.bn_aggr(mv[:, 2 * i:2 * i + 2], stats[:, 6 * i:6 * i + 6]))
                c.last()
                c.then(d.tensor_scalar(ve[:, :], mv[:, :].rearrange("p (n c) -> p n c", c=2)[:, :, 1],
                                       EPS, None, ALU.add))
                dve.wait_ge(ln_rstd, run + 1)
                wait(dve, ln_hi, run)
                for i in range(NB):
                    c.then(d.tensor_scalar(xn32[:, i * D:(i + 1) * D], src(i), mv[:, 2 * i:2 * i + 1],
                                           rstd[:, i:i + 1], ALU.subtract, ALU.mult))

            def x_of(b):
                return lambda i: x1[:, ds(b * (NB * D) + i * D, D)]

            dve.wait_ge(x_first, 16)
            normalise(x_of(0), 0)
            dve.wait_ge(prep_hi, 2)
            low(wvs[:, KD * D:2 * KD * D], tt[:, 0:1024].bitcast(F32), wvs[:, 0:KD * D], WS).then_inc(prep_lo, 1)
            low(rw[:, KD * E:2 * KD * E], tt[:, 1024:1024 + 2 * KD * E].bitcast(F32), rw[:, 0:KD * E],
                WS).then_inc(prep_lo, 1)
            dve.wait_ge(prep_hi, 3)
            low(wm[:, KD * D:2 * KD * D], PT0[:, :], wm[:, 0:KD * D], WS).then_inc(prep_lo, 1)
            dve.wait_ge(small_in, 32)
            for i in range(1, NB):
                ins = d.tensor_copy(biases[:, i * E:(i + 1) * E], biases[:, 0:E])
            ins.then_inc(prep_lo, 1)
            for c in range(CHUNKS):
                w_low(c, c % 2, 0, c)
            dve.wait_ge(x_rest, (B - 1) * 16)
            dve.wait_ge(c_rdy, 1)

            def route(r):
                c = Chain(dve, r_dve, R_STEPS, r)
                b3 = lambda t_: t_[:, :].rearrange("p (n e) -> p n e", n=NB)
                wide = lambda t_: t_[:, :].unsqueeze(2).to_broadcast([P, NB, E])
                dve.wait_ge(lg_mm, r + 1)
                d.scalar_tensor_tensor(out=z[:, :], in0=PT1[:, 0:NB * E], scalar=1.0 / WS, in1=biases[:, :],
                                       op0=ALU.mult, op1=ALU.add).then_inc(lg_read, 1)
                dve.wait_ge(r_exp, r + 1)
                c.then(d.tensor_scalar(pr2[:, :], ez[:, :], 1.0, None, ALU.add)); c.last()
                c.then(d.reciprocal(pr[:, :], pr2[:, :])); c.last()
                cur = pr
                for k in range(TOPK):
                    c.then(d.tensor_reduce(m12[k][:, :], b3(cur), X, ALU.max)); c.last()
                    c.then(d.tensor_tensor(b3(eq), b3(cur), wide(m12[k]), ALU.is_equal)); c.last()
                    c.then(d.tensor_tensor(eq[:, :], eq[:, :], rev[:, :], ALU.mult)); c.last()
                    c.then(d.tensor_reduce(rk[:, :], b3(eq), X, ALU.max)); c.last()
                    c.then(d.tensor_tensor(b3(one_hot[k]), b3(rev), wide(rk), ALU.is_equal)); c.last()
                    if k == 0:
                        c.then(d.scalar_tensor_tensor(out=pr2[:, :], in0=one_hot[0][:, :], scalar=-2.0,
                                                      in1=pr[:, :], op0=ALU.mult, op1=ALU.add)); c.last()
                        cur = pr2
                wait(dve, px_mm, r)
                c.then(d.tensor_tensor(mask[:, :], one_hot[0][:, :], one_hot[1][:, :], ALU.add)); c.last()
                return c

            def weights(r, c):
                c.then(d.tensor_tensor(den[:, :], m12[0][:, :], m12[1][:, :], ALU.add)); c.last()
                c.then(d.reciprocal(rden[:, :], den[:, :])); c.last()
                for k in range(TOPK):
                    ins = d.scalar_tensor_tensor(out=wk[:, ds(r * NB + k * (B * NB), NB)], in0=m12[k][:, :],
                                                 scalar=1.0 / WS, in1=rden[:, :], op0=ALU.mult, op1=ALU.mult)
                c.then(ins)
                c.then(d.tensor_reduce(msum[:, :], mask[:, :].rearrange("p (n e) -> p e n", n=NB), X, ALU.add))
                c.last()
                c.then(d.tensor_tensor(cum[:, :], cum[:, :], msum[:, :], ALU.add)); c.last()
                assert c.k == c.per, c.k

            def places(r):
                dve.wait_ge(px_mm, r + 1)
                d.tensor_tensor(pos[:, :], PT0[:, 0:NB * E], base[:, :], ALU.add).then_inc(px_dve, 1)
                d.tensor_copy(cumh[:, :], cum[:, :]).then_inc(px_dve, 1)
                dve.wait_ge(px_dve, r * 4 + 2)
                wait(dve, scat, 16 * TOPK * NB * r)
                for k in range(TOPK):
                    d.tensor_tensor(pm[:, :], pos[:, :], one_hot[k][:, :], ALU.mult).then_inc(px_dve, 1)
                    dve.wait_ge(px_dve, r * 4 + 3 + k)
                    d.tensor_reduce(sidx[:, k * NB:(k + 1) * NB],
                                    pm[:, :].rearrange("p (n e) -> p n e", n=NB), X, ALU.add).then_inc(sidx_rdy, 1)
                    dve.wait_ge(sidx_rdy, r * 2 + k + 1)

            def ffn_half(t, half):
                g, u = G[half], U[half]
                tb = th[:, half * 512:(half + 1) * 512]
                dve.wait_ge(f_tanh, t * 2 + half + 1)
                d.scalar_tensor_tensor(out=tb, in0=tb, scalar=1.0, in1=g[:, :], op0=ALU.add,
                                       op1=ALU.mult).then_inc(f_sg, 1)
                dve.wait_ge(f_sg, t * 2 + half + 1)
                d.scalar_tensor_tensor(out=tb, in0=tb, scalar=0.5 / (WS * WS), in1=u[:, :], op0=ALU.mult,
                                       op1=ALU.mult).then_inc(f_h, 1)

            def ffn_low(t, half):
                tb = th[:, half * 512:(half + 1) * 512]
                dve.wait_ge(f_hi, t * 2 + half + 1)
                low(h[:, (2 + half) * 512:(3 + half) * 512], tb, h[:, half * 512:(half + 1) * 512]).then_inc(f_lo, 1)

            def add_shared(t, blk0):
                dve.wait_ge(dn_mm, t * 2 + 2)
                o = x1[:, ds(blk0 * D, 2 * D)]
                d.scalar_tensor_tensor(out=o, in0=Y[:, :], scalar=1.0 / WS, in1=o, op0=ALU.mult,
                                       op1=ALU.add).then_inc(y_read, 1)

            def batch(b, first=False, final=False):
                for m in range(KD):
                    dve.wait_ge(t_hi, KD * b + m + 1)
                    low(tt[:, (KD + m) * S:(KD + m + 1) * S], (PT0, PT1)[m][:, :],
                        tt[:, m * S:(m + 1) * S]).then_inc(t_lo, 1)
                if not final:
                    normalise(x_of(b + 1), 2 * b + 1)
                for m in range(2):
                    dve.wait_ge(v_hi, 2 * b + m + 1)
                    low(v[:, (2 + m) * S:(3 + m) * S], (PT2, PT0)[m][:, :],
                        v[:, m * S:(m + 1) * S]).then_inc(v_lo, 1)
                if not first:
                    chain = route(b - 1)
                for c in range(2):
                    w_low(b * CHUNKS + CHUNKS + c, c, b + 1, c)

                def p_low(q):
                    n = (q + 1) * P
                    dve.wait_ge(p_hi, NB * b + q + 1)
                    low(phl[:, (q % 2) * 2 * S + n:(q % 2) * 2 * S + 2 * n], p32[:, (q % 2) * S:(q % 2) * S + n],
                        phl[:, (q % 2) * 2 * S:(q % 2) * 2 * S + n]).then_inc(p_lo, 1)

                for q in range(NB):
                    n = (q + 1) * P
                    dve.wait_ge(s_mm, NB * b + q + 1)
                    if q == 0:
                        wait(dve, s_exp, NB * b)
                    d.tensor_reduce(mx[:, q:q + 1], (PT2, PT0, PT1, PT2)[q][:, 0:n], X, ALU.max).then_inc(s_max, 1)
                    dve.wait_ge(s_max, NB * b + q + 1)
                    d.tensor_scalar(nm[:, q:q + 1], mx[:, q:q + 1], -1.0 / (16.0 * WS), None,
                                    ALU.mult).then_inc(s_nm, 1)
                    if q:
                        p_low(q - 1)
                p_low(NB - 1)
                if not first:
                    weights(b - 1, chain)
                    places(b - 1)
                    for half in range(2):
                        ffn_half(b - 1, half)
                        ffn_low(b - 1, half)
                for c in range(2, CHUNKS):
                    w_low(b * CHUNKS + CHUNKS + c, c % 2, b + 1, c)
                dve.wait_ge(s_exp, NB * b + NB)
                d.tensor_scalar(s16[:, :], sums[:, :], WS, None, ALU.mult).then_inc(sum_dve, 1)
                dve.wait_ge(sum_dve, 2 * b + 1)
                d.reciprocal(rs[:, :], s16[:, :]).then_inc(sum_dve, 1)
                dve.wait_ge(sum_dve, 2 * b + 2)
                for q in range(NB):
                    dve.wait_ge(pv_mm, 2 * b + q // 2 + 1)
                    o = x1[:, ds(b * (NB * D) + q * D, D)]
                    d.scalar_tensor_tensor(out=o, in0=(PT1, PT2)[q // 2][:, (q % 2) * D:(q % 2 + 1) * D],
                                           scalar=rs[:, q:q + 1], in1=o, op0=ALU.mult,
                                           op1=ALU.add).then_inc(x1_put, 1)
                dve.wait_ge(x1_put, NB * b + NB)
                if not final:
                    gate(dve, xn_lo, b + 2, dve_past)
                run = 2 * b + 2 if not final else 2 * b + 1
                normalise(x_of(b), run)
                dve.wait_ge(ln_hi, run + 1)
                r0, r1 = (t_[:, :].rearrange("p (n c) -> p n c", n=NB) for t_ in xrow)
                low(r0[:, :, D:2 * D], blk(xn32), r0[:, :, 0:D]).then_inc(xn2_lo, 1)
                dve.wait_ge(xn2_lo, b + 1)
                wait(dve, scat, 16 * TOPK * NB * b)
                d.tensor_copy(r1[:, :, 0:2 * D], r0[:, :, 0:2 * D]).then_inc(xn2_dup, 1)
                if not first:
                    add_shared(b - 1, b * NB - NB)

            batch(0, first=True)
            with dve.Fori(1, B - 1) as b:
                batch(b)
            batch(B - 1, final=True)
            chain = route(B - 1)
            weights(B - 1, chain)
            places(B - 1)

            c = Chain(dve, tab, T_STEPS, 0)
            r_ = lambda i: tf[0:1, i * E:(i + 1) * E]
            CNT, CF, INC, PREV, VAL, TMP, ONE = (r_(i) for i in range(7))
            t3 = lambda t_: t_[0:1, :].rearrange("p (t e) -> p t e", e=E)
            per_tile = lambda t_: t_.unsqueeze(1).to_broadcast([1, TILES, E])
            t1 = lambda i: p32[0:1, i * TILES:(i + 1) * TILES]
            dve.wait_ge(tio_rdy, 1)
            dve.wait_ge(cnt_mm, 1)
            c.then(d.tensor_copy(CNT, PT2[0:1, 0:E])); c.last()
            c.then(d.tensor_scalar(ti[0:1, :], CNT, float(TT - 1), None, ALU.add)); c.last()
            c.then(d.tensor_single_scalar(ti[0:1, :], ti[0:1, :], TT.bit_length() - 1, ALU.logical_shift_right)); c.last()
            c.then(d.tensor_copy(CF, ti[0:1, :])); c.last()
            c.then(d.memset(ONE, 1.0)); c.last()
            c.then(d.tensor_tensor_scan(INC, ONE, CF, 0.0, ALU.mult, ALU.add)); c.last()
            c.then(d.tensor_tensor(PREV, INC, CF, ALU.subtract)); c.last()
            c.then(d.scalar_tensor_tensor(out=TMP, in0=PREV, scalar=float(TT), in1=CNT, op0=ALU.mult,
                                          op1=ALU.add)); c.last()
            c.then(d.tensor_tensor(VAL, TMP, erow[0:1, 0:E], ALU.add)); c.last()
            c.then(d.tensor_tensor(t3(oh), t3(tio), per_tile(PREV), ALU.is_ge)); c.last()
            c.then(d.tensor_tensor(t3(ot), t3(tio), per_tile(INC), ALU.is_lt)); c.last()
            c.then(d.tensor_tensor(oh[0:1, :], oh[0:1, :], ot[0:1, :], ALU.mult)); c.last()
            c.then(d.tensor_tensor(t3(ot), t3(oh), per_tile(erow[0:1, E:2 * E]), ALU.mult)); c.last()
            c.then(d.tensor_reduce(w_tab[0:1, N0:N1], t3(ot), X, ALU.add)); c.last()
            c.then(d.tensor_tensor(t3(ot), t3(oh), per_tile(VAL), ALU.mult)); c.last()
            c.then(d.tensor_reduce(t1(0), t3(ot), X, ALU.add)); c.last()
            c.then(d.tensor_reduce(t1(1), t3(oh), X, ALU.add)); c.last()
            c.then(d.tensor_tensor(t1(2), t1(1), tneg[0:1, :], ALU.mult)); c.last()
            c.then(d.tensor_tensor(t1(0), t1(0), t1(2), ALU.add)); c.last()
            c.then(d.tensor_scalar(start_tab[0:1, N0:N1], t1(0), float(SPARE), None, ALU.add)); c.last()

            def tile(n, shared_before=None):
                t = n + INLINE
                ffn_half(t, 0)
                if shared_before is not None:
                    add_shared(t - 1, shared_before)
                ffn_low(t, 0)
                ffn_half(t, 1)
                ffn_low(t, 1)

            def combine(b, cnt, slot):
                dve.wait_ge(yin_in[slot], cnt)
                for k in range(TOPK):
                    for n in range(NB):
                        o = x1[:, ds(b * (NB * D) + n * D, D)]
                        if k:
                            dve.wait_ge(c_k0, b * NB + n + 1)
                        d.scalar_tensor_tensor(
                            out=o, in0=yin[slot][:, (n * TOPK + k) * D:(n * TOPK + k + 1) * D],
                            scalar=wk[:, ds(b * NB + (k * B * NB + n), 1)], in1=o, op0=ALU.mult,
                            op1=ALU.add).then_inc(c_put if k else c_k0, 1)

            tile(0)
            with dve.Fori(1, N0 + 1) as n:
                tile(n, n * NB - 2)
            with dve.Fori(N0 + 1, N1 + 1) as n:
                tile(n)
            assert LATE == 5
            for n in range(N1 + 1, NF):
                tile(n, (n - 1 - N1 + EARLY) * NB + 2)
                b = n - N1 - 1
                combine(b, 16 * (b // 2 + 1), b % 2)
            add_shared(NF - 1 + INLINE, (B - 1) * NB)
            dve.wait_ge(y_read, NF + INLINE)
            for b in range(LATE - 1, B):
                combine(b, 16 * (b // 2 + 1), b % 2)

        @block.tensor
        def _(pe):
            mm = nc.tensor.matmul

            pe.wait_ge(qk_in, 48)
            for m in range(KD):
                for k in range(KD):
                    ins = mm(PT0[:, m * D:(m + 1) * D], v[:, 0:1024].bitcast(F32)[:, k * D + m * P:k * D + (m + 1) * P],
                             v[:, 1024:2048].bitcast(F32)[:, k * D:(k + 1) * D], start=(k == 0), stop=(k == KD - 1))
            ins.then_inc(prep_mm, 1)
            pe.wait_ge(prep_lo, 4)
            pe.wait_ge(c_rdy, 1)

            xn4 = xnt[:, :].rearrange("p (n c r) -> p n c r", n=NB, r=P)
            xn24 = xn2t[:, :].rearrange("p (n c r) -> p n c r", n=NB, r=P)

            def gate_up(t, half, j, moving, inline):
                if not inline:
                    pe.wait_ge(f_h, t * 2 - 2 + half + 1)
                for m, o in enumerate((G[half], U[half])):
                    for i in range(2):
                        dst = o[:, i * TT:(i + 1) * TT]
                        if inline:
                            dst = dst.rearrange("p (n r) -> p n r", r=P)
                        cnt = 0
                        for k in range(KD):
                            for ws, ms in PASSES:
                                ins = mm(dst, w_ap(j, ws, m * MAT + k * I + (2 * half + i) * P, P),
                                         moving(ms * KD + k), start=(cnt == 0), stop=(cnt == 3 * KD - 1))
                                cnt += 1
                ins.then_inc(gu_mm, 1)

            def down(t, j):
                wait(pe, y_read, t)
                cnt = 0
                for half in range(2):
                    pe.wait_ge(f_lo, t * 2 + half + 1)
                    for i in (2 * half, 2 * half + 1):
                        for hs, ws in PASSES:
                            for a in range(2):
                                ins = mm(Y[:, a * D:(a + 1) * D],
                                         h[:, (hs * KI + i) * TT + a * P:(hs * KI + i) * TT + (a + 1) * P],
                                         w_ap(j, ws, 2 * MAT + i * D, D), start=(cnt == 0),
                                         stop=(cnt == 6 * KI - 1), skip_group_check=True)
                                cnt += 1
                    ins.then_inc(dn_mm, 1)

            def logits(r, b):
                pe.wait_ge(xn2t_in, r * 64 + 64)
                for i in range(NB):
                    cnt = 0
                    for k in range(KD):
                        for xs, ws in PASSES:
                            ins = mm(PT1[:, i * E:(i + 1) * E], xn24[:, i, xs * KD + k, :],
                                     rw[:, (ws * KD + k) * E:(ws * KD + k + 1) * E],
                                     start=(cnt == 0), stop=(cnt == 3 * KD - 1))
                            cnt += 1
                ins.then_inc(lg_mm, 1)

            def prefix(r):
                pe.wait_ge(r_dve, r * R_STEPS + 14)
                wait(pe, px_dve, r * 4)
                mm(PT0[:, 0:NB * E], tri[:, :], mask[:, :], start=True, stop=False)
                for i in range(NB - 1):
                    n = NB - 1 - i
                    mm(PT0[:, (i + 1) * E:NB * E].rearrange("p (n e) -> p n e", e=E), ones[:, :],
                       mask[:, i * E:(i + 1) * E].unsqueeze(1).to_broadcast([P, n, E]),
                       start=False, stop=False)
                mm(PT0[:, 0:NB * E].rearrange("p (n e) -> p n e", e=E), ones[:, :],
                   cumh[:, :].unsqueeze(1).to_broadcast([P, NB, E]), start=False, stop=True).then_inc(px_mm, 1)

            def batch(b, first=False, final=False):
                pe.wait_ge(xnt_in, b * 16 + 16)
                for m in range(KD):
                    if m == 0:
                        if not first:
                            wait(pe, px_dve, 4 * b - 4)
                    else:
                        wait(pe, x1_put, NB * b - 2)
                    cnt = 0
                    for k in range(KD):
                        for ws, ms in PASSES:
                            ins = mm((PT0, PT1)[m][:, :].rearrange("p (n r) -> p n r", r=P),
                                     wm[:, (ws * KD + k) * D + m * P:(ws * KD + k) * D + (m + 1) * P],
                                     xn4[:, :, ms * KD + k, :], start=(cnt == 0), stop=(cnt == 3 * KD - 1))
                            cnt += 1
                    ins.then_inc(t_mm, 1)
                for m in range(2):
                    if m == 0:
                        wait(pe, x1_put, NB * b)
                    else:
                        pe.wait_ge(t_lo, KD * b + 1)
                    for i in range(2):
                        cnt = 0
                        for k in range(KD):
                            for xs, ws in PASSES:
                                ins = mm((PT2, PT0)[m][:, i * D:(i + 1) * D], xn4[:, 2 * m + i, xs * KD + k, :],
                                         wvs[:, (ws * KD + k) * D:(ws * KD + k + 1) * D],
                                         start=(cnt == 0), stop=(cnt == 3 * KD - 1))
                                cnt += 1
                    ins.then_inc(v_mm, 1)
                if not first:
                    pe.wait_ge(t_lo, KD * b + 2)
                    logits(b - 1, b)
                for q in range(NB):
                    o = (PT2, PT0, PT1, PT2)[q]
                    if q == 0:
                        pe.wait_ge(t_lo, KD * b + 2)
                        pe.wait_ge(v_lo, 2 * b + 1)
                    elif q == 1:
                        pe.wait_ge(v_lo, 2 * b + 2)
                    elif q == 2:
                        wait(pe, lg_read, b)
                    else:
                        pe.wait_ge(s_exp, NB * b + 1)
                    n = q + 1
                    cnt = 0
                    for k in range(KD):
                        for ts, ms in PASSES:
                            lhs = tt[:, (ts * KD + k) * S + q * P:(ts * KD + k) * S + (q + 1) * P]
                            mm(o[:, 0:n * P].rearrange("p (n r) -> p n r", r=P), lhs,
                               xn4[:, 0:n, ms * KD + k, :], start=(cnt == 0), stop=(cnt == 3 * KD - 1))
                            cnt += 1
                    ins = mm(o[:, q * P:n * P], ident[:, :], maskb[:, :], start=False, stop=True,
                             skip_group_check=True)
                    ins.then_inc(s_mm, 1)
                if not first:
                    pe.wait_ge(s_exp, NB * b + 2)
                    prefix(b - 1)
                    for half in range(2):
                        if half == 0:
                            pe.wait_ge(w_lo, CHUNKS)
                        gate_up(b - 1, half, 0, lambda c: xn24[:, 0:2, c, :], True)
                off = 0
                for q in range(NB):
                    if q == 0:
                        pe.wait_ge(v_lo, 2 * b + 2)
                        pe.wait_ge(s_exp, NB * b + 3)
                    elif q == 2:
                        pe.wait_ge(s_exp, NB * b + 4)
                    pe.wait_ge(pt_in[q], b * 16 + 16)
                    cnt, total = 0, 3 * (q + 1)
                    for kb in range(q + 1):
                        for ps, vs in PASSES:
                            ins = mm((PT1, PT2)[q // 2][:, (q % 2) * D:(q % 2 + 1) * D],
                                     ptr[:, off + (ps * (q + 1) + kb) * P:off + (ps * (q + 1) + kb + 1) * P],
                                     v[:, (vs * NB + kb) * D:(vs * NB + kb + 1) * D],
                                     start=(cnt == 0), stop=(cnt == total - 1))
                            cnt += 1
                    off += 2 * (q + 1) * P
                    if q % 2:
                        ins.then_inc(pv_mm, 1)
                if not first:
                    down(b - 1, 0)

            batch(0, first=True)
            with pe.Fori(1, B - 1) as b:
                batch(b)
            batch(B - 1, final=True)
            pe.wait_ge(x1_put, NB * B - 2)
            logits(B - 1, None)
            prefix(B - 1)

            def ffn_moving(slot):
                return lambda c: xt[:, (slot * 4 + c) * TT:(slot * 4 + c + 1) * TT]

            def tile_w(n):
                return pe.value_load(w_tab[0:1, ds(n, 1)], min_val=0, max_val=E)

            def tile(n, slot, cnt, j, j_before):
                t = n + INLINE
                pe.wait_ge(xt_in[slot], cnt)
                gate_up(t, 0, j, ffn_moving(slot), False)
                if j_before is not None:
                    down(t - 1, j_before)
                gate_up(t, 1, j, ffn_moving(slot), False)

            tile(0, 0, 16, 0, None)
            pe.wait_ge(r_dve, B * R_STEPS)
            pe.wait_ge(px_dve, 4 * B)
            mm(PT2[:, 0:E], ones[:, :], cumh[:, :], start=True, stop=True).then_inc(cnt_mm, 1)
            for n in range(1, N0):
                tile(n, n % 2, 16 * (n // 2 + 1), 0, 0)
            pe.wait_ge(tab, T_STEPS)
            pe.wait_ge(w_lo, (E + 1) * CHUNKS)
            j = tile_w(N0)
            tile(N0, N0 % 2, 16 * (N0 // 2 + 1), j, 0)
            assert N0 % 2 == 0 and N1 % 2 == 1
            with pe.Fori(N0 + 1, N1 - 1, 2) as n:
                for s in range(2):
                    j, jb = tile_w(n + s), tile_w(n + (s - 1))
                    slot = (N0 + 1 + s) % 2
                    tile(n + s, slot, (n + s - slot) * 8 + 16, j, jb)
            j = tile_w(N1 - 1)
            tile(N1, N1 % 2, 16 * (N1 // 2 + 1), 0, j)
            for n in range(N1 + 1, NF):
                tile(n, n % 2, 16 * (n // 2 + 1), 0, 0)
            down(NF - 1 + INLINE, 0)


def kernel(**inputs):
    import numpy as np
    import concourse.bacc as bacc
    from concourse.bass_utils import run_bass_kernel_spmd

    g = lambda n: np.asarray(inputs[n])
    nc = bacc.Bacc("TRN2", target_bir_lowering=False, num_devices=1)

    def up(a):
        return a.reshape(KD, P, I).transpose(1, 0, 2).reshape(P, KD * I)

    def down(a):
        return a.reshape(KI, P, D).transpose(1, 0, 2).reshape(P, KI * D)

    cols = [up(g("L0_ffn_shared_gate").T), up(g("L0_ffn_shared_up").T), down(g("L0_ffn_shared_down").T)]
    for e in range(E):
        cols += [up(g("L0_ffn_gate_w")[e]), up(g("L0_ffn_up_w")[e]), down(g("L0_ffn_down_w")[e])]
    arrays = {
        "x": np.ascontiguousarray(g("L0_attn_x").reshape(T, D)),
        "wq_t": np.ascontiguousarray(g("L0_attn_Wq").T),
        "wk_t": np.ascontiguousarray(g("L0_attn_Wk").T),
        "wv": np.ascontiguousarray(g("L0_attn_Wv")),
        "w_all": np.ascontiguousarray(np.concatenate(cols, axis=1)),
        "router": np.ascontiguousarray(g("L0_ffn_router_w").T),
        "bias": np.ascontiguousarray(g("L0_ffn_routing_bias")),
    }
    aps = {n: nc.dram_tensor(n, a.shape, F32, kind="ExternalInput").ap() for n, a in arrays.items()}
    out = nc.dram_tensor("out", (T, D), F32, kind="ExternalOutput").ap()
    build(nc, **aps, out=out)
    r = run_bass_kernel_spmd(nc, [arrays], core_ids=[0])
    return r.results[0]["out"].reshape(B, S, D)
```

```python
from contextlib import ExitStack

import concourse.bass as bass
from concourse import mybir

F32 = mybir.dt.float32
F16 = mybir.dt.float16
BF16 = mybir.dt.bfloat16
I32 = mybir.dt.int32
ALU = mybir.AluOpType
ACT = mybir.ActivationFunctionType
X = mybir.AxisListType.X
ds = bass.ds

P = 128
B, S, D = 8, 512, 256
T = B * S
E, TOPK, I = 8, 2, 512
NB = S // P
KD = D // P
KI = I // P
TT = 256
TILES = (TOPK * T - E) // TT + E
EPS = 1e-5
WS = 16.0
NEG = -1e30

MAT = KD * I
WJ = 3 * MAT
CH = WJ // 4
CHUNKS = 4

REG = T + TT
SPARE = E * REG
ROWS = (E + 1) * REG
RW = 2 * D + 2 * (1 + E)
RC = RW // 2

SHARED = T // TT


def wait(eng, sem, value):
    if isinstance(value, int) and value <= 0:
        return
    eng.wait_ge(sem, value)


def gate(eng, sem, value, passed):
    if isinstance(value, int) and value <= 0:
        return
    eng.wait_ge(sem, value)
    eng.sem_inc(passed, 1)


class Chain:

    def __init__(self, eng, sem, per, run):
        self.eng, self.sem, self.per, self.run, self.k = eng, sem, per, run, 0

    def then(self, ins):
        ins.then_inc(self.sem, 1)
        self.k += 1
        assert self.k <= self.per
        return ins

    def last(self):
        self.eng.wait_ge(self.sem, self.run * self.per + self.k)


def build(nc, x, wq_t, wk_t, wv, w_all, router, bias, out):
    with ExitStack() as ctx:
        ctx.enter_context(nc.allow_low_precision(reason="sums of whole numbers below 2^24, written as int32"))

        def sb(name, width, dt):
            return ctx.enter_context(nc.sbuf_tensor(name, [P, width], dt))

        def sem(name):
            return ctx.enter_context(nc.semaphore(name))

        rows = nc.dram_tensor("rows", [ROWS, RC], I32, kind="Internal").ap()
        w = sb("w", (E + 1) * 2 * WJ, F16)
        x1 = sb("x1", B * NB * D, F32)
        wm = sb("wm", 2 * KD * D, F16)
        wvs = sb("wvs", 2 * KD * D, F16)
        rw = sb("rw", 2 * KD * E, F16)
        biases = sb("biases", NB * E, F32)
        xn32 = sb("xn32", NB * D, F32)
        xnrow = sb("xnrow", 2 * NB * D, F16)
        tt = sb("tt", 2 * KD * S, F16)
        v = sb("v", 2 * NB * D, F16)
        xnt = sb("xnt", 2 * KD * S, F16)
        p32 = sb("p32", 2 * S, F32)
        phl = sb("phl", 2 * 2 * S, F16)
        ptr = sb("ptr", 2 * P * (NB * (NB + 1) // 2), F16)
        xrow = [sb(f"xrow{k}", NB * RW, F16) for k in range(2)]
        xn2t = sb("xn2t", 2 * KD * S, F16)
        th = sb("th", 2 * 2 * TT, F32)
        h = sb("h", 2 * KI * TT, F16)
        wst = sb("wst", 2 * CH, F32)
        ident = sb("ident", P, BF16)
        maskb = sb("maskb", P, BF16)
        tri = sb("tri", P, F16)
        ones = sb("ones", P, F16)
        halves = sb("halves", NB, F32)
        eidx = sb("eidx", E, F32)
        base = sb("base", NB * E, F32)
        tokidx = sb("tokidx", B * NB, I32)
        stats = sb("stats", NB * 6, F32)
        mv = [sb(f"mv{k}", NB * 2, F32) for k in range(2)]
        ve = [sb(f"ve{k}", NB, F32) for k in range(2)]
        rstd = [sb(f"rstd{k}", NB, F32) for k in range(2)]
        nmr = sb("nmr", NB, F32)
        mx = sb("mx", NB, F32)
        nm = sb("nm", NB, F32)
        sums = sb("sums", NB, F32)
        s16 = sb("s16", NB, F32)
        rs = sb("rs", NB, F32)
        z = sb("z", NB * E, F32)
        ez = sb("ez", NB * E, F32)
        pr = sb("pr", NB * E, F32)
        pr2 = sb("pr2", NB * E, F32)
        mx8 = sb("mx8", NB * E, F32)
        ix8 = sb("ix8", NB * E, mybir.dt.uint32)
        idxf = sb("idxf", TOPK * NB, F32)
        one_hot = sb("one_hot", TOPK * NB * E, F32)
        wv_ = sb("wv_", NB * E, F32)
        den = sb("den", NB, F32)
        rden = sb("rden", NB, F32)
        mask = sb("mask", NB * E, F16)
        msum = sb("msum", E, F32)
        cum = sb("cum", E, F32)
        cumh = sb("cumh", E, F16)
        pos = sb("pos", NB * E, F32)
        pm = sb("pm", TOPK * NB * E, F32)
        sidx = sb("sidx", TOPK * NB, I32)
        aux = sb("aux", 2 * 2 * (1 + E), I32)
        start_tab = sb("start_tab", TILES, I32)
        w_tab = sb("w_tab", TILES, I32)
        ti = sb("ti", E, I32)
        tneg = sb("tneg", TILES, F32)
        erow = sb("erow", 2 * E, F32)
        xt = xn2t
        ysb = p32
        tabs = phl[:, :].bitcast(F32)
        tio, oh, ot = (tabs[:, i * TILES * E:(i + 1) * TILES * E] for i in range(3))
        tf = tabs[:, 3 * TILES * E:3 * TILES * E + 7 * E]

        bank = [ctx.enter_context(nc.psum_tensor(f"bank{i}", [P, 512], F32)) for i in range(8)]
        G, U, Y = [bank[0], bank[2]], [bank[1], bank[3]], bank[4]
        PT0, PT1, PT2 = bank[5], bank[6], bank[7]
        T_BANK, V_BANK, S_BANK, PV_BANK = (PT0, PT1), (PT2, U[1]), (G[1], PT0, PT1, PT2), (PT1, PT2)
        LG_BANK, PX_BANK = PT0, PT0

        c_rdy = sem("c_rdy")
        c_dve = sem("c_dve")
        c_pad = sem("c_pad")
        small_in = sem("small_in")
        x_first, x_second, x_rest = sem("x_first"), sem("x_second"), sem("x_rest")
        qk_in = sem("qk_in")
        prep_mm = sem("prep_mm")
        prep_hi = sem("prep_hi")
        prep_lo = sem("prep_lo")
        w_in = [sem("w_in0"), sem("w_in1")]
        w_scaled, w_hi = sem("w_scaled"), sem("w_hi")
        w_lo = sem("w_lo")
        dump_in = sem("dump_in")
        ln1, ln2 = sem("ln1"), sem("ln2")
        rstd1_rdy, rstd2_rdy = sem("rstd1_rdy"), sem("rstd2_rdy")
        xn_put = sem("xn_put")
        xn2_put = sem("xn2_put")
        xn_hi, xn2_hi = sem("xn_hi"), sem("xn2_hi")
        xn_lo = sem("xn_lo")
        xn2_lo = sem("xn2_lo")
        idx_put = sem("idx_put")
        xnt_in = sem("xnt_in")
        xn2t_in = sem("xn2t_in")
        xrow_in = sem("xrow_in")
        t_mm, t_hi, t_lo = sem("t_mm"), sem("t_hi"), sem("t_lo")
        v_mm, v_hi, v_lo = sem("v_mm"), sem("v_hi"), sem("v_lo")
        s_mm = sem("s_mm")
        s_max, s_nm = sem("s_max"), sem("s_nm")
        s_exp, p_hi, p_lo = sem("s_exp"), sem("p_hi"), sem("p_lo")
        pt_in = [sem(f"pt_in{q}") for q in range(NB)]
        pv_mm = sem("pv_mm")
        sum_dve = sem("sum_dve")
        x1_put = sem("x1_put")
        lg_mm, lg_read = sem("lg_mm"), sem("lg_read")
        r_exp, r_dve = sem("r_exp"), sem("r_dve")
        px_mm, px_dve = sem("px_mm"), sem("px_dve")
        sidx_rdy = sem("sidx_rdy")
        rows_in = sem("rows_in")
        cnt_mm = sem("cnt_mm")
        tab = sem("tab")
        tio_rdy = sem("tio_rdy")
        gu_mm = sem("gu_mm")
        f_tanh, f_sg, f_h, f_hi, f_lo = sem("f_tanh"), sem("f_sg"), sem("f_h"), sem("f_hi"), sem("f_lo")
        dn_mm = sem("dn_mm")
        y_read = sem("y_read")
        xt_in = [sem("xt_in0"), sem("xt_in1")]
        ax_in = [sem("ax_in0"), sem("ax_in1")]
        y_out = sem("y_out")
        out_done = sem("out_done")
        sp_past, pool_past, dve_past, act_past = (sem(f"{n}_past") for n in ("sp", "pool", "dve", "act"))

        R_STEPS = 13
        LN1_STEPS, LN2_STEPS = 7, 6
        T_STEPS = 20
        ZERO_ROWS, ROWS_PER = 32, TOPK * NB * 16
        R_MASK = 7

        AW = 2 * (1 + E)

        def blk(t3):
            return t3.rearrange("p (n d) -> p n d", n=NB)

        def w_ap(j, part, off, n):
            return w[:, ds(j * (2 * WJ) + (part * WJ + off), n)]

        PASSES = ((0, 0), (0, 1), (1, 0))

        block = ctx.enter_context(nc.Block())

        @block.sync
        def _(sp):
            sp.dma_start(x1[:, 0:NB * D].rearrange("p (n d) -> p n d", n=NB),
                         x[0:S, :].rearrange("(n p) d -> p n d", p=P)).then_inc(x_first, 16)
            sp.dma_start(v[:, 0:1024].bitcast(F32).rearrange("p (k d) -> p k d", k=KD),
                         wq_t.rearrange("(k p) d -> p k d", p=P)).then_inc(qk_in, 16)
            sp.dma_start(v[:, 1024:2048].bitcast(F32).rearrange("p (k d) -> p k d", k=KD),
                         wk_t.rearrange("(k p) d -> p k d", p=P)).then_inc(qk_in, 16)
            sp.dma_start(tt[:, 0:1024].bitcast(F32).rearrange("p (k d) -> p k d", k=KD),
                         wv.rearrange("(k p) d -> p k d", p=P)).then_inc(qk_in, 16)
            sp.dma_start(tt[:, 1024:1024 + 2 * KD * E].bitcast(F32).rearrange("p (k d) -> p k d", k=KD),
                         router.rearrange("(k p) d -> p k d", p=P)).then_inc(small_in, 16)
            sp.dma_start(biases[:, 0:E], bias.partition_broadcast(P)).then_inc(small_in, 16)

            def w_load(chunk, slot):
                gate(sp, w_lo, chunk - 1, sp_past)
                sp.dma_start(wst[:, slot * CH:(slot + 1) * CH],
                             w_all[:, ds(chunk * CH, CH)]).then_inc(w_in[slot], 16)

            w_load(0, 0)
            w_load(1, 1)

            def x_load(b, done):
                sp.dma_start(blk(x1[:, b * NB * D:(b + 1) * NB * D]),
                             x[b * S:(b + 1) * S, :].rearrange("(n p) d -> p n d", p=P)).then_inc(done, 16)

            x_load(1, x_second)

            def xn_transpose(b):
                gate(sp, s_mm, NB * b, sp_past)
                gate(sp, xn_lo, b + 1, sp_past)
                sp.dma_start_transpose(xnt[:, :].rearrange("p (n r) -> p n r", r=P),
                                       xnrow[:, :]).then_inc(xnt_in, 16)

            xn_transpose(0)
            for b in range(2, B):
                x_load(b, x_rest)
            sp.wait_ge(c_dve, 2)
            sp.dma_start(out[T:T + TT, :].rearrange("(a p) d -> p a d", p=P),
                         p32[:, 0:2 * D].rearrange("p (a d) -> p a d", a=2)).then_inc(dump_in, 16)
            for chunk in (2, 3, 4, 5):
                w_load(chunk, chunk % 2)

            def out_base(b):
                gate(sp, y_read, 2 * b + 2, sp_past)
                sp.dma_start(out[ds(b * S, S), :].rearrange("(n p) d -> p n d", p=P),
                             blk(x1[:, ds(b * (NB * D), NB * D)])).then_inc(out_done, 16)

            def xn2_transpose(b, par, last=False):
                if last:
                    sp.wait_ge(s_mm, NB * B)
                else:
                    gate(sp, gu_mm, 4 * b, sp_past)
                dst = xnt if last else xn2t
                for h2 in range(2):
                    gate(sp, xn2_lo, b * 2 + (h2 + 1), sp_past)
                    sp.dma_start_transpose(
                        dst[:, h2 * 8 * P:(h2 + 1) * 8 * P].rearrange("p (n r) -> p n r", r=P),
                        xnrow[:, h2 * 4 * D:(h2 + 1) * 4 * D]).then_inc(xn2t_in, 16)
                sp.dma_start(xrow[par][:, :].rearrange("p (n c) -> p n c", n=NB)[:, :, 0:2 * D],
                             xnrow[:, :].rearrange("p (n c) -> p n c", n=NB)).then_inc(xrow_in, 16)

            def batch(b, par, first=False, final=False):
                if not first:
                    xn2_transpose(b - 1, 1 - par)
                g = b * CHUNKS + CHUNKS + 2
                off = 0
                for q in range(NB):
                    n = (q + 1) * P
                    gate(sp, pv_mm, 2 * b, sp_past)
                    gate(sp, p_lo, NB * b + q + 1, sp_past)
                    sp.dma_start_transpose(
                        ptr[:, off:off + 2 * n].rearrange("p (n r) -> p n r", r=P),
                        phl[:, (q % 2) * 2 * S:(q % 2) * 2 * S + 2 * n]).then_inc(pt_in[q], 16)
                    off += 2 * n
                w_load(g, 0)
                if not final:
                    xn_transpose(b + 1)
                w_load(g + 1, 1)
                if not final:
                    w_load(g + 2, 0)
                if not final:
                    w_load(g + 3, 1)
                else:
                    xn2_transpose(b, par, last=True)
                if not first:
                    out_base(b - 1)

            batch(0, 0, first=True)
            sp.wait_ge(rows_in, ZERO_ROWS)
            with sp.Fori(1, B - 2, 2) as b:
                for s in range(2):
                    batch(b + s, (1 + s) % 2)
            batch(B - 1, (B - 1) % 2, final=True)

            def load_tile(n, slot, read, used):
                row = sp.value_load(start_tab[0:1, ds(n, 1)], min_val=0, max_val=ROWS - TT)
                gate(sp, gu_mm, read, sp_past)
                sp.dma_start_transpose(
                    xt[:, slot * 4 * TT:(slot + 1) * 4 * TT].rearrange("p (c r) -> p c r", r=TT),
                    rows[ds(row, TT), 0:D].bitcast(F16)).then_inc(xt_in[slot], 16)
                gate(sp, y_out, used, sp_past)
                sp.dma_start(aux[:, slot * AW:(slot + 1) * AW].rearrange("p (a c) -> p a c", a=2),
                             rows[ds(row, TT), D:RC].rearrange("(a p) c -> p a c", p=P)
                             ).then_inc(ax_in[slot], 16)

            sp.wait_ge(tab, T_STEPS)
            sp.wait_ge(rows_in, ZERO_ROWS + B * ROWS_PER)
            load_tile(0, 0, 2 * SHARED - 4, 0)
            load_tile(1, 1, 2 * SHARED - 4, 0)
            out_base(B - 1)
            with sp.Fori(2, TILES - 2, 2) as n:
                for s in range(2):
                    load_tile(n + s, s, n * 2 + (2 * SHARED - 2 + 2 * s), n * 32 - (32 - 32 * s))
            load_tile(TILES - 1, (TILES - 1) % 2, 2 * (SHARED + TILES) - 4, 32 * (TILES - 2))
            sp.wait_ge(y_out, 32 * TILES)

        @block.gpsimd
        def _(pool):
            cc = nc.gpsimd
            steps = [0]

            def const(ins):
                ins.then_inc(c_rdy, 1)
                steps[0] += 1

            def const_wait():
                pool.wait_ge(c_rdy, steps[0])

            const(cc.iota(tokidx[:, :], pattern=[[P, B * NB]], base=0, channel_multiplier=1))
            pool.wait_ge(c_dve, 1)
            cc.iota(xrow[0][:, 0:2 * RW].bitcast(I32).rearrange("p (a c) -> p a c", a=2)[:, :, D],
                    pattern=[[P, 2]], base=T, channel_multiplier=1).then_inc(c_pad, 1)
            const(cc.memset(ident[:, :], 0.0))
            const(cc.memset(maskb[:, :], 0.0))
            const(cc.memset(tri[:, :], 1.0))
            const(cc.memset(ones[:, :], 1.0))
            const(cc.memset(halves[:, :], -0.5))
            const_wait()
            const(cc.affine_select(out=ident[:, :], in_=ident[:, :], compare_op=ALU.not_equal, fill=1.0,
                                   base=0, pattern=[[-1, P]], channel_multiplier=1))
            const(cc.affine_select(out=maskb[:, :], in_=maskb[:, :], compare_op=ALU.is_ge, fill=NEG,
                                   base=0, pattern=[[-1, P]], channel_multiplier=1))
            const(cc.affine_select(out=tri[:, :], in_=tri[:, :], compare_op=ALU.is_gt, fill=0.0,
                                   base=0, pattern=[[1, P]], channel_multiplier=-1))
            imp = dict(allow_small_or_imprecise_dtypes=True)
            const(cc.iota(eidx[:, :], pattern=[[1, E]], base=0, channel_multiplier=0, **imp))
            const(cc.iota(base[:, :].rearrange("p (n e) -> p n e", n=NB), pattern=[[0, NB], [REG, E]],
                          base=TT, channel_multiplier=0, **imp))
            const(cc.iota(tneg[:, :], pattern=[[-TT, TILES]], base=-SPARE, channel_multiplier=0, **imp))
            const(cc.iota(erow[:, 0:E], pattern=[[REG, E]], base=0, channel_multiplier=0, **imp))
            const(cc.iota(erow[:, E:2 * E], pattern=[[1, E]], base=1, channel_multiplier=0, **imp))
            const_wait()

            def rstd_of(i, lns, steps, run, rdy):
                pool.wait_ge(lns, run * steps + 6)
                cc.tensor_tensor(rstd[i][:, :], ve[i][:, :], halves[:, :], ALU.pow).then_inc(rdy, 1)

            def xn_low(b):
                pool.wait_ge(xn_hi, b + 1)
                cc.tensor_tensor(xnrow[:, :].rearrange("p (n c) -> p n c", n=NB)[:, :, D:2 * D], blk(xn32[:, :]),
                                 xnrow[:, :].rearrange("p (n c) -> p n c", n=NB)[:, :, 0:D],
                                 ALU.subtract).then_inc(xn_lo, 1)

            def w_low(g, slot, j, c):
                gate(pool, w_hi, g + 1, pool_past)
                cc.tensor_tensor(w[:, ds(j * (2 * WJ) + (WJ + c * CH), CH)], wst[:, slot * CH:(slot + 1) * CH],
                                 w[:, ds(j * (2 * WJ) + c * CH, CH)], ALU.subtract).then_inc(w_lo, 1)

            def put_idx(b, par):
                if par == 0:
                    pool.wait_ge(rows_in, ZERO_ROWS)
                cc.tensor_copy(xrow[par][:, :].bitcast(I32).rearrange("p (n c) -> p n c", n=NB)[:, :, D],
                               tokidx[:, ds(b * NB, NB)]).then_inc(idx_put, 1)

            def scatter(b, par, k):
                gate(pool, sidx_rdy, b + 1, pool_past)
                gate(pool, xrow_in, b * 16 + 16, pool_past)
                gate(pool, idx_put, b + 1, pool_past)
                for n in range(NB):
                    cc.indirect_dma_start(
                        rows, bass.IndirectOffsetOnAxis(ap=sidx[:, k * NB + n:k * NB + n + 1], axis=0),
                        xrow[par][:, n * RW:(n + 1) * RW].bitcast(I32), None).then_inc(rows_in, 16)

            rstd_of(0, ln1, LN1_STEPS, 0, rstd1_rdy)
            pool.wait_ge(c_dve, 1)
            pool.wait_ge(c_pad, 1)
            for a in range(2):
                zero = xrow[0][:, a * RW:(a + 1) * RW].bitcast(I32)
                cc.dma_start(rows.rearrange("(e r) c -> r e c", e=E + 1)[a * P:(a + 1) * P],
                             zero.unsqueeze(1).to_broadcast([P, E + 1, RC])).then_inc(rows_in, 16)
            xn_low(0)
            for c in range(CHUNKS):
                w_low(c, c % 2, 0, c)

            def batch(b, par, first=False, final=False):
                g = b * CHUNKS + CHUNKS
                if not final:
                    rstd_of(0, ln1, LN1_STEPS, b + 1, rstd1_rdy)
                w_low(g, 0, b + 1, 0)
                if not final:
                    xn_low(b + 1)
                w_low(g + 1, 1, b + 1, 1)
                if not first:
                    put_idx(b - 1, 1 - par)
                if final:
                    rstd_of(1, ln2, LN2_STEPS, b, rstd2_rdy)
                if not first:
                    scatter(b - 1, 1 - par, 0)
                w_low(g + 2, 0, b + 1, 2)
                if not final:
                    rstd_of(1, ln2, LN2_STEPS, b, rstd2_rdy)
                w_low(g + 3, 1, b + 1, 3)
                if not first:
                    scatter(b - 1, 1 - par, 1)

            batch(0, 0, first=True)
            with pool.Fori(1, B - 2, 2) as b:
                for s in range(2):
                    batch(b + s, (1 + s) % 2)
            batch(B - 1, (B - 1) % 2, final=True)
            for q in range(2, NB):
                pool.wait_ge(pt_in[q], 16 * B)
            cc.iota(tio.rearrange("p (t e) -> p t e", t=TILES), pattern=[[1, TILES], [0, E]],
                    base=0, channel_multiplier=0, **imp).then_inc(tio_rdy, 1)
            put_idx(B - 1, (B - 1) % 2)
            for k in range(TOPK):
                scatter(B - 1, (B - 1) % 2, k)

            def y_add(n, slot, cnt):
                gate(pool, y_read, n + (SHARED + 1), pool_past)
                gate(pool, ax_in[slot], cnt, pool_past)
                gate(pool, y_out, n * 32, pool_past)
                for a in range(2):
                    cc.indirect_dma_start(
                        out, bass.IndirectOffsetOnAxis(
                            ap=aux[:, slot * AW + a * (1 + E):slot * AW + a * (1 + E) + 1], axis=0),
                        ysb[:, (slot * 2 + a) * D:(slot * 2 + a + 1) * D], None,
                        compute_op=ALU.add).then_inc(y_out, 16)

            pool.wait_ge(out_done, 16 * B)
            pool.wait_ge(dump_in, 16)
            y_add(0, 0, 16)
            with pool.Fori(1, TILES - 1, 2) as n:
                for s in range(2):
                    y_add(n + s, (1 + s) % 2, n * 8 + (8 + 16 * s))

        @block.scalar
        def _(act):
            a = nc.scalar

            def copy(o, i, scale=1.0):
                return a.activation(o, i, ACT.Copy, scale=scale)

            act.wait_ge(qk_in, 48)
            act.wait_ge(small_in, 32)
            copy(wvs[:, 0:KD * D], tt[:, 0:1024].bitcast(F32), WS).then_inc(prep_hi, 1)
            copy(rw[:, 0:KD * E], tt[:, 1024:1024 + 2 * KD * E].bitcast(F32), WS).then_inc(prep_hi, 1)
            def w_split(g, slot, cnt, j, c):
                piece = wst[:, slot * CH:(slot + 1) * CH]
                act.wait_ge(w_in[slot], cnt)
                copy(piece, piece, WS).then_inc(w_scaled, 1)
                gate(act, w_scaled, g + 1, act_past)
                copy(w[:, ds(j * (2 * WJ) + c * CH, CH)], piece).then_inc(w_hi, 1)

            def xn_normalise(b):
                gate(act, ln1, b * LN1_STEPS + LN1_STEPS, act_past)
                if not (isinstance(b, int) and b < 2):
                    gate(act, xn2_lo, b * 2 - 2, act_past)
                for i in range(NB):
                    ins = a.activation(xn32[:, i * D:(i + 1) * D], x1[:, ds(b * (NB * D) + i * D, D)],
                                       ACT.Identity, scale=rstd[0][:, i:i + 1], bias=nmr[:, i:i + 1])
                ins.then_inc(xn_put, 1)

            def xn_high(b):
                act.wait_ge(xn_put, b + 1)
                if isinstance(b, int) and b < 2:
                    wait(act, xnt_in, 16 * b)
                else:
                    gate(act, xn2t_in, 32 * b - 32, act_past)
                    act.wait_ge(xrow_in, 16 * b - 16)
                copy(xnrow[:, :].rearrange("p (n c) -> p n c", n=NB)[:, :, 0:D], blk(xn32[:, :])).then_inc(xn_hi, 1)

            xn_normalise(0)
            xn_high(0)
            act.wait_ge(prep_mm, 1)
            copy(wm[:, 0:KD * D], PT0[:, :], WS).then_inc(prep_hi, 1)
            for c in range(CHUNKS):
                w_split(c, c % 2, 16 * (c // 2 + 1), 0, c)

            def ffn_half(t, half, inline=False):
                tanh(t, half, inline)
                split_h(t, half, inline)

            def tanh(t, half, inline=False):
                act.wait_ge(gu_mm, t * 2 + half + 1)
                if not inline:
                    act.wait_ge(f_lo, t * 2 - 2 + half + 1)
                a.activation(th[:, half * 512:(half + 1) * 512], G[half][:, :], ACT.Tanh,
                             scale=0.5 / WS).then_inc(f_tanh, 1)

            def split_h(t, half, inline=False):
                act.wait_ge(f_h, t * 2 + half + 1)
                if not inline:
                    act.wait_ge(dn_mm, t * 2 - 2 + half + 1)
                copy(h[:, half * 512:(half + 1) * 512], th[:, half * 512:(half + 1) * 512]).then_inc(f_hi, 1)

            def xn2_high(b, par, h2):
                act.wait_ge(xn2_put, NB * b + 2 * h2 + 2)
                copy(xnrow[:, :].rearrange("p (n c) -> p n c", n=NB)[:, 2 * h2:2 * h2 + 2, 0:D],
                     blk(xn32[:, :])[:, 2 * h2:2 * h2 + 2]).then_inc(xn2_hi, 1)

            def batch(b, par, first=False, final=False):
                for m in range(KD):
                    act.wait_ge(t_mm, KD * b + m + 1)
                    if first:
                        act.wait_ge(prep_lo, 3)
                    wait(act, s_mm, NB * b)
                    copy(tt[:, m * S:(m + 1) * S], T_BANK[m][:, :]).then_inc(t_hi, 1)
                for m in range(2):
                    if not first:
                        xn2_high(b - 1, 1 - par, m)
                    act.wait_ge(v_mm, 2 * b + m + 1)
                    wait(act, pv_mm, 2 * b)
                    copy(v[:, m * S:(m + 1) * S], V_BANK[m][:, :]).then_inc(v_hi, 1)
                w_split(b * CHUNKS + CHUNKS, 0, 32 * b + 48, b + 1, 0)
                for q in range(NB):
                    n = (q + 1) * P
                    sbank = S_BANK[q]
                    act.wait_ge(s_nm, NB * b + q + 1)
                    if q < 2:
                        wait(act, p_lo, NB * b - 2 + q + 1)
                    else:
                        act.wait_ge(p_lo, NB * b + q - 1)
                    if q == 0:
                        wait(act, x1_put, NB * b)
                        if first:
                            act.wait_ge(dump_in, 16)
                    a.activation(p32[:, (q % 2) * S:(q % 2) * S + n], sbank[:, 0:n], ACT.Exp,
                                 bias=nm[:, q:q + 1], scale=1.0 / (16.0 * WS),
                                 accum_out=sums[:, q:q + 1]).then_inc(s_exp, 1)
                    act.wait_ge(s_exp, NB * b + q + 1)
                    if q < 2:
                        wait(act, pt_in[q + 2], 16 * b)
                    else:
                        act.wait_ge(pt_in[q - 2], 16 * b + 16)
                    copy(phl[:, (q % 2) * 2 * S:(q % 2) * 2 * S + n],
                         p32[:, (q % 2) * S:(q % 2) * S + n]).then_inc(p_hi, 1)
                if not first:
                    act.wait_ge(lg_read, b)
                    a.activation(ez[:, :], z[:, :], ACT.Exp, scale=-1.0).then_inc(r_exp, 1)
                    ffn_half(2 * b - 2, 0, inline=True)
                    tanh(2 * b - 2, 1, inline=True)
                if not final:
                    xn_normalise(b + 1)
                if not first:
                    split_h(2 * b - 2, 1, inline=True)
                if not final:
                    xn_high(b + 1)
                w_split(b * CHUNKS + (CHUNKS + 1), 1, 32 * b + 48, b + 1, 1)
                if not first and not final:
                    ffn_half(2 * b - 1, 0)
                    ffn_half(2 * b - 1, 1)
                w_split(b * CHUNKS + (CHUNKS + 2), 0, 32 * b + 64, b + 1, 2)
                w_split(b * CHUNKS + (CHUNKS + 3), 1, 32 * b + 64, b + 1, 3)

            batch(0, 0, first=True)
            with act.Fori(1, B - 2, 2) as b:
                for s in range(2):
                    batch(b + s, (1 + s) % 2)
            batch(B - 1, (B - 1) % 2, final=True)
            ffn_half(SHARED - 3, 0)
            for h2 in range(2):
                xn2_high(B - 1, (B - 1) % 2, h2)
            ffn_half(SHARED - 3, 1)
            act.wait_ge(lg_read, B)
            a.activation(ez[:, :], z[:, :], ACT.Exp, scale=-1.0).then_inc(r_exp, 1)
            for t in (SHARED - 2, SHARED - 1):
                for half in range(2):
                    ffn_half(t, half)

            def y_copy(n, slot, cnt, free):
                j = act.value_load(w_tab[0:1, ds(n, 1)], min_val=0, max_val=E)
                gate(act, ax_in[slot], cnt, act_past)
                gate(act, y_out, free, act_past)
                gate(act, dn_mm, n * 2 + (2 * SHARED + 2), act_past)
                for c in range(2):
                    ins = a.activation(ysb[:, (slot * 2 + c) * D:(slot * 2 + c + 1) * D], Y[:, c * D:(c + 1) * D],
                                       ACT.Copy, scale=aux[:, :].bitcast(F32)[
                                           :, ds(j + (slot * AW + c * (1 + E)), 1)])
                ins.then_inc(y_read, 1)

            def tile(n, before=None):
                ffn_half(n + SHARED, 0)
                if before is not None:
                    y_copy(n - 1, *before)
                ffn_half(n + SHARED, 1)

            act.wait_ge(tab, T_STEPS)
            tile(0)
            tile(1, (0, 16, 0))
            tile(2, (1, 16, 0))
            with act.Fori(3, TILES - 1, 2) as n:
                for s in range(2):
                    tile(n + s, (s, n * 8 + 8, n * 32 - (64 - 32 * s)))
            y_copy(TILES - 1, (TILES - 1) % 2, 16 * ((TILES - 1) // 2 + 1), 32 * (TILES - 2))

        @block.vector
        def _(dve):
            d = nc.vector
            d.memset(xrow[0][:, 0:2 * RW], 0.0).then_inc(c_dve, 1)
            d.memset(p32[:, 0:2 * D], 0.0).then_inc(c_dve, 1)
            d.memset(cum[:, :], 0.0).then_inc(c_dve, 1)
            d.memset(cumh[:, :], 0.0).then_inc(c_dve, 1)

            def low(o, full, hi, scale=None):
                if scale is None:
                    return d.tensor_tensor(o, full, hi, ALU.subtract)
                return d.scalar_tensor_tensor(out=o, in0=full, scalar=scale, in1=hi, op0=ALU.mult, op1=ALU.subtract)

            def stats_of(i, lns, steps, run, src, chain=None):
                c = Chain(dve, lns, steps, run)
                for n in range(NB):
                    ins = d.bn_stats(stats[:, 6 * n:6 * n + 6], src(n))
                c.then(ins)
                aggregate(i, c)
                return c

            def aggregate(i, c):
                gate(dve, c.sem, c.run * c.per + 1, dve_past)
                for n in range(NB):
                    c.then(d.bn_aggr(mv[i][:, 2 * n:2 * n + 2], stats[:, 6 * n:6 * n + 6]))
                c.last()
                c.then(d.tensor_scalar(ve[i][:, :], mv[i][:, :].rearrange("p (n c) -> p n c", c=2)[:, :, 1],
                                       EPS, None, ALU.add))

            def shift_of(run, c):
                dve.wait_ge(rstd1_rdy, run + 1)
                c.then(d.scalar_tensor_tensor(out=nmr[:, :], in0=mv[0][:, :].rearrange("p (n c) -> p n c", c=2)[:, :, 0],
                                              scalar=-1.0, in1=rstd[0][:, :], op0=ALU.mult, op1=ALU.mult))

            def x_of(b):
                return lambda i: x1[:, ds(b * (NB * D) + i * D, D)]

            dve.wait_ge(x_first, 16)
            shift_of(0, stats_of(0, ln1, LN1_STEPS, 0, x_of(0)))
            dve.wait_ge(prep_hi, 2)
            low(wvs[:, KD * D:2 * KD * D], tt[:, 0:1024].bitcast(F32), wvs[:, 0:KD * D], WS).then_inc(prep_lo, 1)
            low(rw[:, KD * E:2 * KD * E], tt[:, 1024:1024 + 2 * KD * E].bitcast(F32), rw[:, 0:KD * E],
                WS).then_inc(prep_lo, 1)
            dve.wait_ge(prep_hi, 3)
            low(wm[:, KD * D:2 * KD * D], PT0[:, :], wm[:, 0:KD * D], WS).then_inc(prep_lo, 1)
            dve.wait_ge(small_in, 32)
            for i in range(1, NB):
                ins = d.tensor_copy(biases[:, i * E:(i + 1) * E], biases[:, 0:E])
            ins.then_inc(prep_lo, 1)
            dve.wait_ge(x_second, 16)
            dve.wait_ge(c_rdy, 1)

            b3 = lambda t_: t_[:, :].rearrange("p (n e) -> p n e", e=E)

            def read_logits(r):
                dve.wait_ge(lg_mm, r + 1)
                d.scalar_tensor_tensor(out=z[:, :], in0=LG_BANK[:, 0:NB * E], scalar=1.0 / WS, in1=biases[:, :],
                                       op0=ALU.mult, op1=ALU.add).then_inc(lg_read, 1)

            def route(r):
                c = Chain(dve, r_dve, R_STEPS, r)
                dve.wait_ge(r_exp, r + 1)
                c.then(d.tensor_scalar(pr2[:, :], ez[:, :], 1.0, None, ALU.add)); c.last()
                c.then(d.reciprocal(pr[:, :], pr2[:, :]))
                gate(dve, r_dve, r * R_STEPS + c.k, dve_past)
                for n in range(NB):
                    ins = d.max(mx8[:, n * E:(n + 1) * E], pr[:, n * E:(n + 1) * E])
                c.then(ins)
                gate(dve, r_dve, r * R_STEPS + c.k, dve_past)
                for n in range(NB):
                    ins = d.max_index(ix8[:, n * E:(n + 1) * E], mx8[:, n * E:(n + 1) * E], pr[:, n * E:(n + 1) * E])
                c.then(ins); c.last()
                return c

            def one_hots(r, c):
                c.then(d.tensor_copy(idxf[:, :].rearrange("p (k n) -> p k n", k=TOPK),
                                     ix8[:, :].rearrange("p (n e) -> p e n", e=E)[:, 0:TOPK, :])); c.last()
                c.then(d.tensor_tensor(b3(one_hot), eidx[:, :].unsqueeze(1).to_broadcast([P, TOPK * NB, E]),
                                       idxf[:, :].unsqueeze(2).to_broadcast([P, TOPK * NB, E]), ALU.is_equal)); c.last()
                c.then(d.tensor_tensor(mask[:, :], one_hot[:, 0:NB * E], one_hot[:, NB * E:2 * NB * E], ALU.add))
                assert c.k == R_MASK

            def weights(r, par, c):
                mxk = mx8[:, :].rearrange("p (n e) -> p e n", e=E)
                c.last()
                c.then(d.tensor_tensor(den[:, :], mxk[:, 0, :], mxk[:, 1, :], ALU.add))
                c.then(d.tensor_tensor(wv_[:, :], pr[:, :], mask[:, :], ALU.mult)); c.last()
                c.then(d.reciprocal(rden[:, :], den[:, :]))
                c.then(d.tensor_reduce(msum[:, :], mask[:, :].rearrange("p (n e) -> p e n", n=NB), X, ALU.add)); c.last()
                if par == 0:
                    dve.wait_ge(rows_in, ZERO_ROWS)
                c.then(d.scalar_tensor_tensor(
                    out=xrow[par][:, :].bitcast(F32).rearrange("p (n c) -> p n c", n=NB)[:, :, D + 1:RC],
                    in0=b3(wv_), scalar=1.0 / WS, in1=rden[:, :].unsqueeze(2).to_broadcast([P, NB, E]),
                    op0=ALU.mult, op1=ALU.mult))
                c.then(d.tensor_tensor(cum[:, :], cum[:, :], msum[:, :], ALU.add)); c.last()
                assert c.k == c.per, c.k

            def places(r):
                dve.wait_ge(px_mm, r + 1)
                d.tensor_tensor(pos[:, :], PX_BANK[:, 0:NB * E], base[:, :], ALU.add).then_inc(px_dve, 1)
                d.tensor_copy(cumh[:, :], cum[:, :]).then_inc(px_dve, 1)
                dve.wait_ge(px_dve, r * 3 + 2)
                d.tensor_tensor(pm[:, :].rearrange("p (k m) -> p k m", k=TOPK),
                                pos[:, :].unsqueeze(1).to_broadcast([P, TOPK, NB * E]),
                                one_hot[:, :].rearrange("p (k m) -> p k m", k=TOPK), ALU.mult).then_inc(px_dve, 1)
                dve.wait_ge(px_dve, r * 3 + 3)
                dve.wait_ge(rows_in, ROWS_PER * r + ZERO_ROWS)
                d.tensor_reduce(sidx[:, :], b3(pm), X, ALU.add).then_inc(sidx_rdy, 1)

            def ffn_half(t, half):
                g, u = G[half], U[half]
                tb = th[:, half * 512:(half + 1) * 512]
                dve.wait_ge(f_tanh, t * 2 + half + 1)
                d.scalar_tensor_tensor(out=tb, in0=tb, scalar=1.0, in1=g[:, :], op0=ALU.add,
                                       op1=ALU.mult).then_inc(f_sg, 1)
                dve.wait_ge(f_sg, t * 2 + half + 1)
                d.scalar_tensor_tensor(out=tb, in0=tb, scalar=0.5 / (WS * WS), in1=u[:, :], op0=ALU.mult,
                                       op1=ALU.mult).then_inc(f_h, 1)

            def ffn_low(t, half):
                tb = th[:, half * 512:(half + 1) * 512]
                dve.wait_ge(f_hi, t * 2 + half + 1)
                low(h[:, (2 + half) * 512:(3 + half) * 512], tb, h[:, half * 512:(half + 1) * 512]).then_inc(f_lo, 1)

            def add_shared(t, blk0):
                dve.wait_ge(dn_mm, t * 2 + 2)
                o = x1[:, ds(blk0 * D, 2 * D)]
                d.scalar_tensor_tensor(out=o, in0=Y[:, :], scalar=1.0 / WS, in1=o, op0=ALU.mult,
                                       op1=ALU.add).then_inc(y_read, 1)

            def ln2_put(b, h2):
                if h2 == 0:
                    dve.wait_ge(xn_lo, b + 2 if not isinstance(b, int) or b < B - 1 else B)
                    dve.wait_ge(rstd2_rdy, b + 1)
                for i in (2 * h2, 2 * h2 + 1):
                    d.tensor_scalar(xn32[:, i * D:(i + 1) * D], x_of(b)(i), mv[1][:, 2 * i:2 * i + 1],
                                    rstd[1][:, i:i + 1], ALU.subtract, ALU.mult).then_inc(xn2_put, 1)

            def ln2_low(b, par, h2):
                dve.wait_ge(xn2_hi, 2 * b + h2 + 1)
                r0 = xnrow[:, :].rearrange("p (n c) -> p n c", n=NB)[:, 2 * h2:2 * h2 + 2]
                low(r0[:, :, D:2 * D], blk(xn32[:, :])[:, 2 * h2:2 * h2 + 2], r0[:, :, 0:D]).then_inc(xn2_lo, 1)

            def batch(b, par, first=False, final=False):
                if not first:
                    ln2_put(b - 1, 0)
                for m in range(KD):
                    dve.wait_ge(t_hi, KD * b + m + 1)
                    low(tt[:, (KD + m) * S:(KD + m + 1) * S], T_BANK[m][:, :],
                        tt[:, m * S:(m + 1) * S]).then_inc(t_lo, 1)
                if not first:
                    ln2_put(b - 1, 1)
                for m in range(2):
                    if not first:
                        ln2_low(b - 1, 1 - par, m)
                    dve.wait_ge(v_hi, 2 * b + m + 1)
                    low(v[:, (2 + m) * S:(3 + m) * S], V_BANK[m][:, :],
                        v[:, m * S:(m + 1) * S]).then_inc(v_lo, 1)
                if not final:
                    c1 = stats_of(0, ln1, LN1_STEPS, b + 1, x_of(b + 1))

                def p_low(q):
                    n = (q + 1) * P
                    dve.wait_ge(p_hi, NB * b + q + 1)
                    low(phl[:, (q % 2) * 2 * S + n:(q % 2) * 2 * S + 2 * n], p32[:, (q % 2) * S:(q % 2) * S + n],
                        phl[:, (q % 2) * 2 * S:(q % 2) * 2 * S + n]).then_inc(p_lo, 1)

                for q in range(NB):
                    n = (q + 1) * P
                    dve.wait_ge(s_mm, NB * b + q + 1)
                    if q == 0:
                        wait(dve, s_exp, NB * b)
                    d.tensor_reduce(mx[:, q:q + 1], S_BANK[q][:, 0:n], X, ALU.max).then_inc(s_max, 1)
                    dve.wait_ge(s_max, NB * b + q + 1)
                    d.tensor_scalar(nm[:, q:q + 1], mx[:, q:q + 1], -1.0 / (16.0 * WS), None,
                                    ALU.mult).then_inc(s_nm, 1)
                    if q:
                        p_low(q - 1)
                    if q == 1 and not final:
                        shift_of(b + 1, c1)
                if not first:
                    read_logits(b - 1)
                p_low(NB - 1)
                if not first:
                    ta, tb = 2 * b - 2, 2 * b - 1
                    ffn_half(ta, 0)
                    chain = route(b - 1)
                    ffn_low(ta, 0)
                    ffn_half(ta, 1)
                    one_hots(b - 1, chain)
                    ffn_low(ta, 1)
                    weights(b - 1, 1 - par, chain)
                    if not final:
                        ffn_half(tb, 0)
                    places(b - 1)
                    add_shared(ta, b * NB - NB)
                    if not final:
                        ffn_low(tb, 0)
                dve.wait_ge(s_exp, NB * b + NB)
                d.tensor_scalar(s16[:, :], sums[:, :], WS, None, ALU.mult).then_inc(sum_dve, 1)
                dve.wait_ge(sum_dve, 2 * b + 1)
                d.reciprocal(rs[:, :], s16[:, :]).then_inc(sum_dve, 1)
                if not first and not final:
                    ffn_half(tb, 1)
                c2 = Chain(dve, ln2, LN2_STEPS, b)
                dve.wait_ge(sum_dve, 2 * b + 2)
                for h2 in range(2):
                    dve.wait_ge(pv_mm, 2 * b + h2 + 1)
                    for q in (2 * h2, 2 * h2 + 1):
                        o = x1[:, ds(b * (NB * D) + q * D, D)]
                        d.scalar_tensor_tensor(out=o, in0=PV_BANK[h2][:, (q % 2) * D:(q % 2 + 1) * D],
                                               scalar=rs[:, q:q + 1], in1=o, op0=ALU.mult,
                                               op1=ALU.add).then_inc(x1_put, 1)
                    if h2 == 0 and not first and not final:
                        ffn_low(tb, 1)
                    gate(dve, x1_put, NB * b + 2 * h2 + 2, dve_past)
                    for q in (2 * h2, 2 * h2 + 1):
                        ins = d.bn_stats(stats[:, 6 * q:6 * q + 6], x_of(b)(q))
                c2.then(ins)
                aggregate(1, c2)
                if not first:
                    if not final:
                        add_shared(tb, b * NB - (NB - 2))

            batch(0, 0, first=True)
            dve.wait_ge(x_rest, (B - 2) * 16)
            with dve.Fori(1, B - 2, 2) as b:
                for s in range(2):
                    batch(b + s, (1 + s) % 2)
            batch(B - 1, (B - 1) % 2, final=True)
            ffn_half(SHARED - 3, 0)
            for h2 in range(2):
                ln2_put(B - 1, h2)
            ffn_low(SHARED - 3, 0)
            for h2 in range(2):
                ln2_low(B - 1, (B - 1) % 2, h2)
            ffn_half(SHARED - 3, 1)
            ffn_low(SHARED - 3, 1)
            read_logits(B - 1)
            chain = route(B - 1)
            one_hots(B - 1, chain)
            add_shared(SHARED - 3, T // P - NB - 2)
            ffn_half(SHARED - 2, 0)
            weights(B - 1, (B - 1) % 2, chain)
            places(B - 1)
            ffn_low(SHARED - 2, 0)
            ffn_half(SHARED - 2, 1)
            ffn_low(SHARED - 2, 1)

            c = Chain(dve, tab, T_STEPS, 0)
            r_ = lambda i: tf[0:1, i * E:(i + 1) * E]
            CNT, CF, INC, PREV, VAL, TMP, ONE = (r_(i) for i in range(7))
            t3 = lambda t_: t_[0:1, :].rearrange("p (t e) -> p t e", e=E)
            per_tile = lambda t_: t_.unsqueeze(1).to_broadcast([1, TILES, E])
            t1 = lambda i: p32[0:1, i * TILES:(i + 1) * TILES]
            dve.wait_ge(tio_rdy, 1)
            dve.wait_ge(cnt_mm, 1)
            c.then(d.tensor_copy(CNT, PT2[0:1, 0:E])); c.last()
            c.then(d.tensor_scalar(ti[0:1, :], CNT, float(TT - 1), None, ALU.add)); c.last()
            c.then(d.tensor_single_scalar(ti[0:1, :], ti[0:1, :], TT.bit_length() - 1, ALU.logical_shift_right)); c.last()
            c.then(d.tensor_copy(CF, ti[0:1, :])); c.last()
            c.then(d.memset(ONE, 1.0)); c.last()
            c.then(d.tensor_tensor_scan(INC, ONE, CF, 0.0, ALU.mult, ALU.add)); c.last()
            c.then(d.tensor_tensor(PREV, INC, CF, ALU.subtract)); c.last()
            c.then(d.scalar_tensor_tensor(out=TMP, in0=PREV, scalar=float(TT), in1=CNT, op0=ALU.mult,
                                          op1=ALU.add)); c.last()
            c.then(d.tensor_tensor(VAL, TMP, erow[0:1, 0:E], ALU.add)); c.last()
            c.then(d.tensor_tensor(t3(oh), t3(tio), per_tile(PREV), ALU.is_ge)); c.last()
            c.then(d.tensor_tensor(t3(ot), t3(tio), per_tile(INC), ALU.is_lt)); c.last()
            c.then(d.tensor_tensor(oh[0:1, :], oh[0:1, :], ot[0:1, :], ALU.mult)); c.last()
            c.then(d.tensor_tensor(t3(ot), t3(oh), per_tile(erow[0:1, E:2 * E]), ALU.mult)); c.last()
            c.then(d.tensor_reduce(w_tab[0:1, :], t3(ot), X, ALU.add)); c.last()
            c.then(d.tensor_tensor(t3(ot), t3(oh), per_tile(VAL), ALU.mult)); c.last()
            c.then(d.tensor_reduce(t1(0), t3(ot), X, ALU.add)); c.last()
            c.then(d.tensor_reduce(t1(1), t3(oh), X, ALU.add)); c.last()
            c.then(d.tensor_tensor(t1(2), t1(1), tneg[0:1, :], ALU.mult)); c.last()
            c.then(d.tensor_tensor(t1(0), t1(0), t1(2), ALU.add)); c.last()
            c.then(d.tensor_scalar(start_tab[0:1, :], t1(0), float(SPARE), None, ALU.add)); c.last()

            ffn_half(SHARED - 1, 0)
            add_shared(SHARED - 2, T // P - 4)
            ffn_low(SHARED - 1, 0)
            ffn_half(SHARED - 1, 1)
            ffn_low(SHARED - 1, 1)

            def tile(n, shared_before=False):
                t = n + SHARED
                ffn_half(t, 0)
                if shared_before:
                    add_shared(SHARED - 1, T // P - 2)
                ffn_low(t, 0)
                ffn_half(t, 1)
                ffn_low(t, 1)

            tile(0, True)
            with dve.Fori(1, TILES) as n:
                tile(n)

        @block.tensor
        def _(pe):
            mm = nc.tensor.matmul

            pe.wait_ge(qk_in, 48)
            for m in range(KD):
                for k in range(KD):
                    ins = mm(PT0[:, m * D:(m + 1) * D], v[:, 0:1024].bitcast(F32)[:, k * D + m * P:k * D + (m + 1) * P],
                             v[:, 1024:2048].bitcast(F32)[:, k * D:(k + 1) * D], start=(k == 0), stop=(k == KD - 1))
            ins.then_inc(prep_mm, 1)
            pe.wait_ge(prep_lo, 4)
            pe.wait_ge(c_rdy, 1)

            xn4 = xnt[:, :].rearrange("p (n c r) -> p n c r", n=NB, r=P)
            xn24 = xn2t[:, :].rearrange("p (n c r) -> p n c r", n=NB, r=P)

            def gate_up(t, half, j, moving, shape3, covered=False):
                if not covered:
                    pe.wait_ge(f_h, t * 2 - 2 + half + 1)
                for m, o in enumerate((G[half], U[half])):
                    for i in range(2):
                        dst = o[:, i * TT:(i + 1) * TT]
                        if shape3:
                            dst = dst.rearrange("p (n r) -> p n r", r=P)
                        cnt = 0
                        for k in range(KD):
                            for ws, ms in PASSES:
                                ins = mm(dst, w_ap(j, ws, m * MAT + k * I + (2 * half + i) * P, P),
                                         moving(ms * KD + k), start=(cnt == 0), stop=(cnt == 3 * KD - 1))
                                cnt += 1
                ins.then_inc(gu_mm, 1)

            def down(t, j, covered=False):
                if not covered:
                    pe.wait_ge(y_read, t)
                cnt = 0
                for half in range(2):
                    pe.wait_ge(f_lo, t * 2 + half + 1)
                    for i in (2 * half, 2 * half + 1):
                        for hs, ws in PASSES:
                            for a in range(2):
                                ins = mm(Y[:, a * D:(a + 1) * D],
                                         h[:, (hs * KI + i) * TT + a * P:(hs * KI + i) * TT + (a + 1) * P],
                                         w_ap(j, ws, 2 * MAT + i * D, D), start=(cnt == 0),
                                         stop=(cnt == 6 * KI - 1), skip_group_check=True)
                                cnt += 1
                    ins.then_inc(dn_mm, 1)

            def logits(r, last=False):
                pe.wait_ge(xn2t_in, r * 32 + 32)
                src = xn4 if last else xn24
                for i in range(NB):
                    cnt = 0
                    for k in range(KD):
                        for xs, ws in PASSES:
                            ins = mm(LG_BANK[:, i * E:(i + 1) * E], src[:, i, xs * KD + k, :],
                                     rw[:, (ws * KD + k) * E:(ws * KD + k + 1) * E],
                                     start=(cnt == 0), stop=(cnt == 3 * KD - 1))
                            cnt += 1
                ins.then_inc(lg_mm, 1)

            def prefix(r):
                pe.wait_ge(r_dve, r * R_STEPS + R_MASK)
                mm(PX_BANK[:, 0:NB * E], tri[:, :], mask[:, :], start=True, stop=False)
                for i in range(NB - 1):
                    n = NB - 1 - i
                    mm(PX_BANK[:, (i + 1) * E:NB * E].rearrange("p (n e) -> p n e", e=E), ones[:, :],
                       mask[:, i * E:(i + 1) * E].unsqueeze(1).to_broadcast([P, n, E]),
                       start=False, stop=False)
                mm(PX_BANK[:, 0:NB * E].rearrange("p (n e) -> p n e", e=E), ones[:, :],
                   cumh[:, :].unsqueeze(1).to_broadcast([P, NB, E]), start=False, stop=True).then_inc(px_mm, 1)

            def pv(b):
                off = 0
                for q in range(NB):
                    pe.wait_ge(pt_in[q], b * 16 + 16)
                    cnt, total = 0, 3 * (q + 1)
                    for kb in range(q + 1):
                        for ps, vs in PASSES:
                            ins = mm(PV_BANK[q // 2][:, (q % 2) * D:(q % 2 + 1) * D],
                                     ptr[:, off + (ps * (q + 1) + kb) * P:off + (ps * (q + 1) + kb + 1) * P],
                                     v[:, (vs * NB + kb) * D:(vs * NB + kb + 1) * D],
                                     start=(cnt == 0), stop=(cnt == total - 1))
                            cnt += 1
                    off += 2 * (q + 1) * P
                    if q % 2:
                        ins.then_inc(pv_mm, 1)

            def half_batch(src4, i):
                return lambda c: src4[:, 2 * i:2 * i + 2, c, :]

            def batch(b, first=False, final=False):
                pe.wait_ge(xnt_in, b * 16 + 16)
                wait(pe, x1_put, NB * b - 2)
                for m in range(KD):
                    cnt = 0
                    for k in range(KD):
                        for ws, ms in PASSES:
                            ins = mm(T_BANK[m][:, :].rearrange("p (n r) -> p n r", r=P),
                                     wm[:, (ws * KD + k) * D + m * P:(ws * KD + k) * D + (m + 1) * P],
                                     xn4[:, :, ms * KD + k, :], start=(cnt == 0), stop=(cnt == 3 * KD - 1))
                            cnt += 1
                    ins.then_inc(t_mm, 1)
                for m in range(2):
                    if m == 0:
                        wait(pe, x1_put, NB * b)
                    for i in range(2):
                        cnt = 0
                        for k in range(KD):
                            for xs, ws in PASSES:
                                ins = mm(V_BANK[m][:, i * D:(i + 1) * D], xn4[:, 2 * m + i, xs * KD + k, :],
                                         wvs[:, (ws * KD + k) * D:(ws * KD + k + 1) * D],
                                         start=(cnt == 0), stop=(cnt == 3 * KD - 1))
                                cnt += 1
                    ins.then_inc(v_mm, 1)
                for q in range(NB):
                    o = S_BANK[q]
                    if q == 0:
                        pe.wait_ge(t_lo, KD * b + 2)
                    elif q == 3:
                        pe.wait_ge(v_lo, 2 * b + 1)
                    n = q + 1
                    cnt = 0
                    for k in range(KD):
                        for ts, ms in PASSES:
                            lhs = tt[:, (ts * KD + k) * S + q * P:(ts * KD + k) * S + (q + 1) * P]
                            mm(o[:, 0:n * P].rearrange("p (n r) -> p n r", r=P), lhs,
                               xn4[:, 0:n, ms * KD + k, :], start=(cnt == 0), stop=(cnt == 3 * KD - 1))
                            cnt += 1
                    mm(o[:, q * P:n * P], ident[:, :], maskb[:, :], start=False, stop=True,
                       skip_group_check=True).then_inc(s_mm, 1)
                if not first:
                    pe.wait_ge(s_exp, NB * b + 2)
                    logits(b - 1)
                    pe.wait_ge(w_lo, CHUNKS)
                    ta, tb = 2 * b - 2, 2 * b - 1
                    gate_up(ta, 0, 0, half_batch(xn24, 0), True, covered=True)
                    pe.wait_ge(v_lo, 2 * b + 2)
                    pe.wait_ge(s_exp, NB * b + 1)
                    gate_up(ta, 1, 0, half_batch(xn24, 0), True, covered=True)
                    if not final:
                        gate_up(tb, 0, 0, half_batch(xn24, 1), True)
                    down(ta, 0, covered=True)
                    prefix(b - 1)
                    if not final:
                        gate_up(tb, 1, 0, half_batch(xn24, 1), True)
                pe.wait_ge(v_lo, 2 * b + 2)
                pe.wait_ge(s_exp, NB * b + 4)
                pv(b)
                if not first:
                    if final:
                        gate_up(tb, 0, 0, half_batch(xn24, 1), True)
                        gate_up(tb, 1, 0, half_batch(xn24, 1), True)
                    down(tb, 0)

            batch(0, first=True)
            with pe.Fori(1, B - 1) as b:
                batch(b)
            batch(B - 1, final=True)
            pe.wait_ge(x1_put, NB * B)
            logits(B - 1, last=True)
            ta, tb = SHARED - 2, SHARED - 1
            gate_up(ta, 0, 0, half_batch(xn4, 0), True)
            prefix(B - 1)
            gate_up(ta, 1, 0, half_batch(xn4, 0), True)
            pe.wait_ge(px_dve, 3 * B)
            mm(PT2[:, 0:E], ones[:, :], cumh[:, :], start=True, stop=True).then_inc(cnt_mm, 1)
            gate_up(tb, 0, 0, half_batch(xn4, 1), True)
            down(ta, 0)
            gate_up(tb, 1, 0, half_batch(xn4, 1), True)

            def tile_w(n):
                return pe.value_load(w_tab[0:1, ds(n, 1)], min_val=0, max_val=E)

            def tile(n, slot, cnt, j, j_before):
                t = n + SHARED
                moving = lambda c: xt[:, (slot * 4 + c) * TT:(slot * 4 + c + 1) * TT]
                pe.wait_ge(xt_in[slot], cnt)
                gate_up(t, 0, j, moving, False)
                down(t - 1, j_before)
                gate_up(t, 1, j, moving, False)

            pe.wait_ge(tab, T_STEPS)
            pe.wait_ge(w_lo, (E + 1) * CHUNKS)
            tile(0, 0, 16, tile_w(0), 0)
            with pe.Fori(1, TILES - 1, 2) as n:
                for s in range(2):
                    j, jb = tile_w(n + s), tile_w(n + (s - 1))
                    tile(n + s, (1 + s) % 2, n * 8 + (8 + 16 * s), j, jb)
            down(SHARED + TILES - 1, tile_w(TILES - 1))


def kernel(**inputs):
    import numpy as np
    import concourse.bacc as bacc
    from concourse.bass_utils import run_bass_kernel_spmd

    g = lambda n: np.asarray(inputs[n])
    nc = bacc.Bacc("TRN2", target_bir_lowering=False, num_devices=1)

    def up(a):
        return a.reshape(KD, P, I).transpose(1, 0, 2).reshape(P, KD * I)

    def down(a):
        return a.reshape(KI, P, D).transpose(1, 0, 2).reshape(P, KI * D)

    cols = [up(g("L0_ffn_shared_gate").T), up(g("L0_ffn_shared_up").T), down(g("L0_ffn_shared_down").T)]
    for e in range(E):
        cols += [up(g("L0_ffn_gate_w")[e]), up(g("L0_ffn_up_w")[e]), down(g("L0_ffn_down_w")[e])]
    arrays = {
        "x": np.ascontiguousarray(g("L0_attn_x").reshape(T, D)),
        "wq_t": np.ascontiguousarray(g("L0_attn_Wq").T),
        "wk_t": np.ascontiguousarray(g("L0_attn_Wk").T),
        "wv": np.ascontiguousarray(g("L0_attn_Wv")),
        "w_all": np.ascontiguousarray(np.concatenate(cols, axis=1)),
        "router": np.ascontiguousarray(g("L0_ffn_router_w").T),
        "bias": np.ascontiguousarray(g("L0_ffn_routing_bias")),
    }
    aps = {n: nc.dram_tensor(n, a.shape, F32, kind="ExternalInput").ap() for n, a in arrays.items()}
    out = nc.dram_tensor("out", (T + TT, D), F32, kind="ExternalOutput").ap()
    build(nc, **aps, out=out)
    r = run_bass_kernel_spmd(nc, [arrays], core_ids=[0])
    return r.results[0]["out"][:T].reshape(B, S, D)
```

```python
from contextlib import ExitStack

import concourse.bass as bass
from concourse import mybir

F32 = mybir.dt.float32
F16 = mybir.dt.float16
BF16 = mybir.dt.bfloat16
I32 = mybir.dt.int32
ALU = mybir.AluOpType
ACT = mybir.ActivationFunctionType
X = mybir.AxisListType.X
ds = bass.ds

P = 128
B, S, D = 8, 512, 256
T = B * S
E, TOPK, I = 8, 2, 512
NB = S // P
KD = D // P
KI = I // P
NP = NB * (NB + 1) // 2
TT = 256
BLOCKS = (TOPK * T - E) // P + E
PAIRS = (TOPK * T // P - E) // 2
SINGLES = BLOCKS - 2 * PAIRS
TAB = PAIRS + SINGLES
EPS = 1e-5
WS = 16.0
NEG = -1e30
FAR = float(1 << 20)

MAT = KD * I
WJ = 3 * MAT
CH = WJ // 4
CHUNKS = 4

REG = T + P
SPARE = E * REG
ROWS = (E + 1) * REG
RW = 2 * D + 2 * (1 + E)
RC = RW // 2

SHARED = T // TT


FFN0 = SHARED + PAIRS
assert PAIRS % 2 == 0 and SINGLES % 4 == 3 and PAIRS // 2 - 1 <= SINGLES


def wait(eng, sem, value):
    if isinstance(value, int) and value <= 0:
        return
    eng.wait_ge(sem, value)


def gate(eng, sem, value, passed):
    if isinstance(value, int) and value <= 0:
        return
    eng.wait_ge(sem, value)
    eng.sem_inc(passed, 1)


class Chain:

    def __init__(self, eng, sem, per, run):
        self.eng, self.sem, self.per, self.run, self.k = eng, sem, per, run, 0

    def then(self, ins):
        ins.then_inc(self.sem, 1)
        self.k += 1
        assert self.k <= self.per
        return ins

    def last(self):
        self.eng.wait_ge(self.sem, self.run * self.per + self.k)


def build(nc, x, wq_t, wk_t, wv, w_all, router, bias, out):
    with ExitStack() as ctx:
        ctx.enter_context(nc.allow_low_precision(reason="sums of whole numbers below 2^24, written as int32"))

        def sb(name, width, dt):
            return ctx.enter_context(nc.sbuf_tensor(name, [P, width], dt))

        def sem(name):
            return ctx.enter_context(nc.semaphore(name))

        rows = nc.dram_tensor("rows", [ROWS, RC], I32, kind="Internal").ap()
        w = sb("w", (E + 1) * 2 * WJ, F16)
        x1 = sb("x1", B * NB * D, F32)
        wm = sb("wm", 2 * KD * D, F16)
        wvs = sb("wvs", 2 * KD * D, F16)
        rw = sb("rw", 2 * KD * E, F16)
        biases = sb("biases", NB * E, F32)
        xn32 = sb("xn32", NB * D, F32)
        xnrow = sb("xnrow", 2 * NB * D, F16)
        tt = sb("tt", 2 * KD * S, F16)
        v = sb("v", 2 * NB * D, F16)
        xnt = sb("xnt", 2 * KD * S, F16)
        p32 = sb("p32", 2 * S, F32)
        phl = sb("phl", 4 * S, F16)
        ptr = sb("ptr", 2 * NP * P, F16)
        xrow = [sb(f"xrow{k}", NB * RW, F16) for k in range(2)]
        xn2t = sb("xn2t", 2 * KD * S, F16)
        th = sb("th", 2 * 2 * TT, F32)
        h = sb("h", 2 * KI * TT, F16)
        wst = sb("wst", 2 * CH, F32)
        ident = sb("ident", P, BF16)
        maskb = sb("maskb", P, BF16)
        tri = sb("tri", P, F16)
        ones = sb("ones", P, F16)
        halves = sb("halves", NB, F32)
        eidx = sb("eidx", E, F32)
        base = sb("base", NB * E, F32)
        tokidx = sb("tokidx", B * NB, I32)
        stats = sb("stats", NB * 6, F32)
        mv = [sb(f"mv{k}", NB * 2, F32) for k in range(2)]
        ve = [sb(f"ve{k}", NB, F32) for k in range(2)]
        rstd = [sb(f"rstd{k}", NB, F32) for k in range(2)]
        nmr = sb("nmr", NB, F32)
        mx = sb("mx", NB, F32)
        nm = sb("nm", NB, F32)
        sums = sb("sums", NB, F32)
        s16 = sb("s16", NB, F32)
        rs = sb("rs", NB, F32)
        z = sb("z", NB * E, F32)
        ez = sb("ez", NB * E, F32)
        pr = sb("pr", NB * E, F32)
        pr2 = sb("pr2", NB * E, F32)
        mx8 = sb("mx8", NB * E, F32)
        ix8 = sb("ix8", NB * E, mybir.dt.uint32)
        idxf = sb("idxf", TOPK * NB, F32)
        one_hot = sb("one_hot", TOPK * NB * E, F32)
        wv_ = sb("wv_", NB * E, F32)
        den = sb("den", NB, F32)
        rden = sb("rden", NB, F32)
        mask = sb("mask", NB * E, F16)
        msum = sb("msum", E, F32)
        cum = sb("cum", E, F32)
        cumh = sb("cumh", E, F16)
        pos = sb("pos", NB * E, F32)
        pm = sb("pm", TOPK * NB * E, F32)
        sidx = sb("sidx", TOPK * NB, I32)
        aux = sb("aux", 2 * 2 * (1 + E), I32)
        start_tab = sb("start_tab", TAB + 2, I32)
        w_tab = sb("w_tab", TAB + 2, I32)
        ti = sb("ti", 2 * E, I32)
        tneg = sb("tneg", TAB, F32)
        xt = xn2t
        aux_b = xn32
        ht = v
        ysb = p32
        tabs = phl[:, :].bitcast(F32)
        tio, oh, ot = (tabs[:, i * PAIRS * E:(i + 1) * PAIRS * E] for i in range(3))
        tf = tabs[:, 3 * PAIRS * E:3 * PAIRS * E + 10 * E]
        tsum = tabs[:, 3 * PAIRS * E + 10 * E:3 * PAIRS * E + 10 * E + 2 * PAIRS]

        bank = [ctx.enter_context(nc.psum_tensor(f"bank{i}", [P, 512], F32)) for i in range(8)]
        YB = (bank[4], bank[5])
        G, U, Y = [bank[0], bank[2]], [bank[1], bank[3]], bank[4]
        PT0, PT1, PT2 = bank[5], bank[6], bank[7]
        T_BANK, V_BANK, S_BANK, PV_BANK = (PT0, PT1), (PT2, U[1]), (G[1], PT0, PT1, PT2), (PT1, PT2)
        PX_BANK = PT0
        YS_BANK = (Y, G[0])

        c_rdy = sem("c_rdy")
        c_dve = sem("c_dve")
        c_pad = sem("c_pad")
        small_in = sem("small_in")
        x_first, x_second = sem("x_first"), sem("x_second")
        x_early, x_late = sem("x_early"), sem("x_late")
        qk_in = sem("qk_in")
        prep_mm = sem("prep_mm")
        prep_hi = sem("prep_hi")
        prep_lo = sem("prep_lo")
        w_in = [sem("w_in0"), sem("w_in1")]
        w_scaled, w_hi = sem("w_scaled"), sem("w_hi")
        w_lo = sem("w_lo")
        dump_in = sem("dump_in")
        ln1, ln2 = sem("ln1"), sem("ln2")
        rstd1_rdy, rstd2_rdy = sem("rstd1_rdy"), sem("rstd2_rdy")
        xn_put = sem("xn_put")
        xn2_put = sem("xn2_put")
        xn_hi, xn2_hi = sem("xn_hi"), sem("xn2_hi")
        xn_lo = sem("xn_lo")
        xn2_lo = sem("xn2_lo")
        idx_put = sem("idx_put")
        xnt_in = sem("xnt_in")
        xn2t_in = sem("xn2t_in")
        xrow_in = sem("xrow_in")
        t_mm, t_hi, t_lo = sem("t_mm"), sem("t_hi"), sem("t_lo")
        v_mm, v_hi, v_lo = sem("v_mm"), sem("v_hi"), sem("v_lo")
        s_mm = sem("s_mm")
        s_max, s_nm = sem("s_max"), sem("s_nm")
        s_exp, p_hi, p_lo = sem("s_exp"), sem("p_hi"), sem("p_lo")
        pt_in = [sem(f"pt_in{q}") for q in range(NB)]
        pv_mm = sem("pv_mm")
        sum_dve = sem("sum_dve")
        x1_put = sem("x1_put")
        lg_mm, lg_read = sem("lg_mm"), sem("lg_read")
        r_exp, r_dve = sem("r_exp"), sem("r_dve")
        px_mm, px_dve = sem("px_mm"), sem("px_dve")
        sidx_rdy = sem("sidx_rdy")
        rows_in = sem("rows_in")
        cnt_mm = sem("cnt_mm")
        tab, tab2 = sem("tab"), sem("tab2")
        tio_rdy = sem("tio_rdy")
        gu_mm = sem("gu_mm")
        f_tanh, f_sg, f_h, f_hi, f_lo = sem("f_tanh"), sem("f_sg"), sem("f_h"), sem("f_hi"), sem("f_lo")
        dn_mm = sem("dn_mm")
        y_read = sem("y_read")
        xt_in = [sem("xt_in0"), sem("xt_in1")]
        xb_in = [sem(f"xb_in{i}") for i in range(4)]
        ax_in = [sem("ax_in0"), sem("ax_in1")]
        aux_b_in, now_put = sem("aux_b_in"), sem("now_put")
        ht_in = [sem("ht_in0"), sem("ht_in1")]
        y_out = sem("y_out")
        out_done = sem("out_done")
        sp_past, pool_past, dve_past, act_past = (sem(f"{n}_past") for n in ("sp", "pool", "dve", "act"))

        R_STEPS = 13
        LN1_STEPS, LN2_STEPS = 7, 6
        T_STEPS, T2_STEPS = 19, 16
        ZERO_ROWS, ROWS_PER = 16, TOPK * NB * 16
        R_MASK = 7

        AW = 2 * (1 + E)

        def at(q):
            return q * (q + 1) // 2

        P32_AT, PHL_AT = (0, P, 4 * P, 0), (0, 8 * P, 2 * P, 8 * P)

        def sidx_of(r):
            return stats[:, 0:TOPK * NB].bitcast(I32) if isinstance(r, int) and r == B - 1 else sidx[:, :]

        def blk(t3):
            return t3.rearrange("p (n d) -> p n d", n=NB)

        def w_ap(j, part, off, n):
            return w[:, ds(j * (2 * WJ) + (part * WJ + off), n)]

        PASSES = ((0, 0), (0, 1), (1, 0))

        block = ctx.enter_context(nc.Block())

        @block.sync
        def _(sp):
            sp.dma_start(x1[:, 0:NB * D].rearrange("p (n d) -> p n d", n=NB),
                         x[0:S, :].rearrange("(n p) d -> p n d", p=P)).then_inc(x_first, 16)
            sp.dma_start(v[:, 0:1024].bitcast(F32).rearrange("p (k d) -> p k d", k=KD),
                         wq_t.rearrange("(k p) d -> p k d", p=P)).then_inc(qk_in, 16)
            sp.dma_start(v[:, 1024:2048].bitcast(F32).rearrange("p (k d) -> p k d", k=KD),
                         wk_t.rearrange("(k p) d -> p k d", p=P)).then_inc(qk_in, 16)
            sp.dma_start(tt[:, 0:1024].bitcast(F32).rearrange("p (k d) -> p k d", k=KD),
                         wv.rearrange("(k p) d -> p k d", p=P)).then_inc(qk_in, 16)
            sp.dma_start(tt[:, 1024:1024 + 2 * KD * E].bitcast(F32).rearrange("p (k d) -> p k d", k=KD),
                         router.rearrange("(k p) d -> p k d", p=P)).then_inc(small_in, 16)
            sp.dma_start(biases[:, 0:E], bias.partition_broadcast(P)).then_inc(small_in, 16)

            def w_load(chunk, slot):
                gate(sp, w_lo, chunk - 1, sp_past)
                sp.dma_start(wst[:, slot * CH:(slot + 1) * CH],
                             w_all[:, ds(chunk * CH, CH)]).then_inc(w_in[slot], 16)

            w_load(0, 0)
            w_load(1, 1)

            def x_load(b, done):
                sp.dma_start(blk(x1[:, b * NB * D:(b + 1) * NB * D]),
                             x[b * S:(b + 1) * S, :].rearrange("(n p) d -> p n d", p=P)).then_inc(done, 16)

            x_load(1, x_second)

            def xn_transpose(b):
                gate(sp, s_mm, NB * b, sp_past)
                gate(sp, xn_lo, b + 1, sp_past)
                sp.dma_start_transpose(xnt[:, :].rearrange("p (n r) -> p n r", r=P),
                                       xnrow[:, :]).then_inc(xnt_in, 16)

            xn_transpose(0)
            sp.wait_ge(c_dve, 2)
            sp.dma_start(out[T:T + P, :], p32[:, 0:D]).then_inc(dump_in, 16)
            for chunk in (2, 3):
                w_load(chunk, chunk % 2)

            def out_base(b):
                gate(sp, y_read, 2 * b + 2, sp_past)
                sp.dma_start(out[ds(b * S, S), :].rearrange("(n p) d -> p n d", p=P),
                             blk(x1[:, ds(b * (NB * D), NB * D)])).then_inc(out_done, 16)

            def xn2_transpose(b, par, last=False):
                if last:
                    sp.wait_ge(s_mm, NB * B)
                else:
                    gate(sp, gu_mm, 4 * b, sp_past)
                dst = xnt if last else xn2t
                for h2 in range(2):
                    gate(sp, xn2_lo, b * 2 + (h2 + 1), sp_past)
                    sp.dma_start_transpose(
                        dst[:, h2 * 8 * P:(h2 + 1) * 8 * P].rearrange("p (n r) -> p n r", r=P),
                        xnrow[:, h2 * 4 * D:(h2 + 1) * 4 * D]).then_inc(xn2t_in, 16)
                if last:
                    sp.wait_ge(rows_in, ZERO_ROWS + (B - 2) * ROWS_PER)
                sp.dma_start(xrow[par][:, :].rearrange("p (n c) -> p n c", n=NB)[:, :, 0:2 * D],
                             xnrow[:, :].rearrange("p (n c) -> p n c", n=NB)).then_inc(xrow_in, 16)

            def batch(b, par, first=False, final=False):
                g = b * CHUNKS + CHUNKS
                for q in range(NB):
                    part = slice(2 * P * at(q), 2 * P * at(q + 1))
                    gate(sp, pv_mm, 2 * b, sp_past)
                    gate(sp, p_lo, NB * b + q + 1, sp_past)
                    sp.dma_start_transpose(ptr[:, part].rearrange("p (n r) -> p n r", r=P),
                                           phl[:, PHL_AT[q]:PHL_AT[q] + 2 * P * (q + 1)]).then_inc(pt_in[q], 16)
                if first:
                    xn_transpose(1)
                w_load(g, 0)
                w_load(g + 1, 1)
                if first:
                    for later in (2, 3, 4):
                        x_load(later, x_early)
                elif par and not final:
                    sp.dma_start(blk(x1[:, ds(b * (NB * D // 2) + 9 * (NB * D // 2), NB * D)]),
                                 x[ds(b * (S // 2) + 9 * (S // 2), S), :].rearrange("(n p) d -> p n d", p=P)
                                 ).then_inc(x_late, 16)
                if not first and not final:
                    xn_transpose(b + 1)
                w_load(g + 2, 0)
                w_load(g + 3, 1)
                if first:
                    sp.wait_ge(rows_in, ZERO_ROWS)
                xn2_transpose(b, par, last=final)
                if not first:
                    out_base(b - 1)

            batch(0, 0, first=True)
            with sp.Fori(1, B - 2, 2) as b:
                for s in range(2):
                    batch(b + s, (1 + s) % 2)
            batch(B - 1, (B - 1) % 2, final=True)

            def free_rows(read):
                gate(sp, gu_mm, read, sp_past)

            def free_aux(used):
                gate(sp, y_out, used, sp_past)

            def load_tile(n, slot, read, used):
                row = sp.value_load(start_tab[0:1, ds(n, 1)], min_val=0, max_val=ROWS - TT)
                free_rows(read)
                sp.dma_start_transpose(
                    xt[:, slot * 4 * TT:(slot + 1) * 4 * TT].rearrange("p (c r) -> p c r", r=TT),
                    rows[ds(row, TT), 0:D].bitcast(F16)).then_inc(xt_in[slot], 16)
                free_aux(used)
                sp.dma_start(aux[:, slot * AW:(slot + 1) * AW].rearrange("p (a c) -> p a c", a=2),
                             rows[ds(row, TT), D:RC].rearrange("(a p) c -> p a c", p=P)
                             ).then_inc(ax_in[slot], 16)

            def load_block(b, q):
                row = sp.value_load(start_tab[0:1, ds(b + PAIRS, 1)], min_val=0, max_val=ROWS - P)
                if isinstance(b, int) and b < 4:
                    free_rows(2 * FFN0 - 2 + 2 * (q // 2))
                else:
                    free_rows(b + (2 * FFN0 - 3))
                sp.dma_start_transpose(
                    xt[:, q * 4 * P:(q + 1) * 4 * P].rearrange("p (c r) -> p c r", r=P),
                    rows[ds(row, P), 0:D].bitcast(F16)).then_inc(xb_in[q], 16)

            def h_transpose(b, slot):
                if not isinstance(b, int) or b > 1:
                    gate(sp, dn_mm, b + (2 * FFN0 - 1), sp_past)
                gate(sp, f_lo, b + (2 * FFN0 + 1), sp_past)
                sp.dma_start_transpose(
                    ht[:, slot * 8 * P:(slot + 1) * 8 * P].rearrange("p (c r) -> p c r", r=P),
                    h[:, slot * 4 * TT:(slot + 1) * 4 * TT]).then_inc(ht_in[slot], 16)

            sp.wait_ge(tab, T_STEPS)
            sp.wait_ge(rows_in, ZERO_ROWS + B * ROWS_PER)
            load_tile(0, 0, 2 * SHARED - 4, 0)
            load_tile(1, 1, 2 * SHARED - 4, 0)
            out_base(B - 1)
            with sp.Fori(2, PAIRS, 2) as n:
                for s in range(2):
                    load_tile(n + s, s, n * 2 + (2 * SHARED - 2 + 2 * s), n * 32 - (32 - 32 * s))
            sp.wait_ge(tab2, T2_STEPS)
            for b in range(4):
                load_block(b, b)
            for b in range(3):
                h_transpose(b, b % 2)
                load_block(b + 4, b)
            with sp.Fori(0, SINGLES // 4 - 1) as i:
                for s in range(3, 7):
                    h_transpose(i * 4 + s, s % 2)
                    load_block(i * 4 + (s + 4), s % 4)
            for b in range(SINGLES - 4, SINGLES):
                h_transpose(b, b % 2)
            sp.wait_ge(y_out, 32 * PAIRS + 16 * SINGLES)

        @block.gpsimd
        def _(pool):
            cc = nc.gpsimd
            steps = [0]

            def const(ins):
                ins.then_inc(c_rdy, 1)
                steps[0] += 1

            def const_wait():
                pool.wait_ge(c_rdy, steps[0])

            const(cc.iota(tokidx[:, :], pattern=[[P, B * NB]], base=0, channel_multiplier=1))
            pool.wait_ge(c_dve, 1)
            cc.iota(xrow[0][:, 0:RW].bitcast(I32)[:, D:D + 1], pattern=[[0, 1]], base=T,
                    channel_multiplier=1).then_inc(c_pad, 1)
            const(cc.memset(ident[:, :], 0.0))
            const(cc.memset(maskb[:, :], 0.0))
            const(cc.memset(tri[:, :], 1.0))
            const(cc.memset(ones[:, :], 1.0))
            const(cc.memset(halves[:, :], -0.5))
            const_wait()
            const(cc.affine_select(out=ident[:, :], in_=ident[:, :], compare_op=ALU.not_equal, fill=1.0,
                                   base=0, pattern=[[-1, P]], channel_multiplier=1))
            const(cc.affine_select(out=maskb[:, :], in_=maskb[:, :], compare_op=ALU.is_ge, fill=NEG,
                                   base=0, pattern=[[-1, P]], channel_multiplier=1))
            const(cc.affine_select(out=tri[:, :], in_=tri[:, :], compare_op=ALU.is_gt, fill=0.0,
                                   base=0, pattern=[[1, P]], channel_multiplier=-1))
            imp = dict(allow_small_or_imprecise_dtypes=True)
            const(cc.iota(eidx[:, :], pattern=[[1, E]], base=0, channel_multiplier=0, **imp))
            const(cc.iota(base[:, :].rearrange("p (n e) -> p n e", n=NB), pattern=[[0, NB], [REG, E]],
                          base=P, channel_multiplier=0, **imp))
            const(cc.iota(tneg[:, 0:PAIRS], pattern=[[-TT, PAIRS]], base=0, channel_multiplier=0, **imp))
            const(cc.iota(tneg[:, PAIRS:TAB], pattern=[[-P, SINGLES]], base=0, channel_multiplier=0, **imp))
            const_wait()

            def rstd_of(i, lns, steps, run, rdy):
                pool.wait_ge(lns, run * steps + 6)
                cc.tensor_tensor(rstd[i][:, :], ve[i][:, :], halves[:, :], ALU.pow).then_inc(rdy, 1)

            def xn_low(b):
                pool.wait_ge(xn_hi, b + 1)
                cc.tensor_tensor(xnrow[:, :].rearrange("p (n c) -> p n c", n=NB)[:, :, D:2 * D], blk(xn32[:, :]),
                                 xnrow[:, :].rearrange("p (n c) -> p n c", n=NB)[:, :, 0:D],
                                 ALU.subtract).then_inc(xn_lo, 1)

            def w_low(g, slot, j, c):
                gate(pool, w_hi, g + 1, pool_past)
                cc.tensor_tensor(w[:, ds(j * (2 * WJ) + (WJ + c * CH), CH)], wst[:, slot * CH:(slot + 1) * CH],
                                 w[:, ds(j * (2 * WJ) + c * CH, CH)], ALU.subtract).then_inc(w_lo, 1)

            def put_idx(b, par):
                if par == 0:
                    pool.wait_ge(rows_in, ZERO_ROWS)
                cc.tensor_copy(xrow[par][:, :].bitcast(I32).rearrange("p (n c) -> p n c", n=NB)[:, :, D],
                               tokidx[:, ds(b * NB, NB)]).then_inc(idx_put, 1)

            def scatter(b, par, k):
                gate(pool, sidx_rdy, b + 1, pool_past)
                gate(pool, xrow_in, b * 16 + 16, pool_past)
                gate(pool, idx_put, b + 1, pool_past)
                for n in range(NB):
                    cc.indirect_dma_start(
                        rows, bass.IndirectOffsetOnAxis(ap=sidx_of(b)[:, k * NB + n:k * NB + n + 1], axis=0),
                        xrow[par][:, n * RW:(n + 1) * RW].bitcast(I32), None).then_inc(rows_in, 16)

            rstd_of(0, ln1, LN1_STEPS, 0, rstd1_rdy)
            pool.wait_ge(xn_put, 1)
            rstd_of(0, ln1, LN1_STEPS, 1, rstd1_rdy)
            for c in range(2):
                w_low(c, c, 0, c)
            pool.wait_ge(c_dve, 1)
            pool.wait_ge(c_pad, 1)
            cc.dma_start(rows.rearrange("(e r) c -> r e c", e=E + 1)[0:P],
                         xrow[0][:, 0:RW].bitcast(I32).unsqueeze(1).to_broadcast([P, E + 1, RC])
                         ).then_inc(rows_in, 16)

            def batch(b, par, first=False, final=False):
                g = b * CHUNKS + CHUNKS
                if first:
                    xn_low(1)
                w_low(g - 2, 0, b, 2)
                if not first and not final:
                    rstd_of(0, ln1, LN1_STEPS, b + 1, rstd1_rdy)
                w_low(g - 1, 1, b, 3)
                if not first and not final:
                    xn_low(b + 1)
                if first:
                    rstd_of(1, ln2, LN2_STEPS, b, rstd2_rdy)
                w_low(g, 0, b + 1, 0)
                w_low(g + 1, 1, b + 1, 1)
                if not first:
                    put_idx(b - 1, 1 - par)
                    rstd_of(1, ln2, LN2_STEPS, b, rstd2_rdy)
                    for k in range(TOPK):
                        scatter(b - 1, 1 - par, k)

            batch(0, 0, first=True)
            with pool.Fori(1, B - 2, 2) as b:
                for s in range(2):
                    batch(b + s, (1 + s) % 2)
            batch(B - 1, (B - 1) % 2, final=True)
            for q in range(NB):
                pool.wait_ge(pt_in[q], 16 * B)
            cc.iota(tio.rearrange("p (t e) -> p t e", t=PAIRS), pattern=[[1, PAIRS], [0, E]],
                    base=0, channel_multiplier=0, **imp).then_inc(tio_rdy, 1)
            put_idx(B - 1, (B - 1) % 2)
            for k in range(TOPK):
                scatter(B - 1, (B - 1) % 2, k)
            w_low(E * CHUNKS + 2, 0, E, 2)
            w_low(E * CHUNKS + 3, 1, E, 3)

            def y_add(n, slot, cnt):
                gate(pool, y_read, n + (SHARED + 1), pool_past)
                gate(pool, ax_in[slot], cnt, pool_past)
                gate(pool, y_out, n * 32, pool_past)
                for a in range(2):
                    cc.indirect_dma_start(
                        out, bass.IndirectOffsetOnAxis(
                            ap=aux[:, slot * AW + a * (1 + E):slot * AW + a * (1 + E) + 1], axis=0),
                        ysb[:, (slot * 2 + a) * D:(slot * 2 + a + 1) * D], None,
                        compute_op=ALU.add).then_inc(y_out, 16)

            def load_aux(b):
                row = pool.value_load(start_tab[0:1, ds(b + PAIRS, 1)], min_val=0, max_val=ROWS - P)
                cc.dma_start(aux_b[:, ds(b * (1 + E), 1 + E)],
                             rows[ds(row, P), D:RC].bitcast(F32)).then_inc(aux_b_in, 16)

            def y_add_block(b, slot):
                now = aux[:, slot * AW:slot * AW + 1]
                cc.tensor_copy(now, aux_b[:, :].bitcast(I32)[:, ds(b * (1 + E), 1)]).then_inc(now_put, 1)
                gate(pool, now_put, b + 1, pool_past)
                gate(pool, y_read, b + (FFN0 + 1), pool_past)
                gate(pool, y_out, b * 16 + 32 * PAIRS, pool_past)
                cc.indirect_dma_start(
                    out, bass.IndirectOffsetOnAxis(ap=now, axis=0),
                    ysb[:, slot * 2 * D:(slot * 2 + 1) * D], None, compute_op=ALU.add).then_inc(y_out, 16)

            pool.wait_ge(out_done, 16 * B)
            pool.wait_ge(dump_in, 16)
            y_add(0, 0, 16)
            pool.wait_ge(tab2, T2_STEPS)
            with pool.Fori(1, PAIRS // 2) as i:
                y_add(i * 2 - 1, 1, i * 16)
                load_aux(i - 1)
                y_add(i * 2, 0, i * 16 + 16)
            for b in range(PAIRS // 2 - 1, SINGLES):
                load_aux(b)
            y_add(PAIRS - 1, 1, 8 * PAIRS)
            pool.wait_ge(aux_b_in, 16 * SINGLES)
            with pool.Fori(0, SINGLES - 1, 2) as b:
                for s in range(2):
                    y_add_block(b + s, s)
            y_add_block(SINGLES - 1, 0)

        @block.scalar
        def _(act):
            a = nc.scalar

            def copy(o, i, scale=1.0):
                return a.activation(o, i, ACT.Copy, scale=scale)

            def w_split(g, slot, cnt, j, c):
                piece = wst[:, slot * CH:(slot + 1) * CH]
                act.wait_ge(w_in[slot], cnt)
                copy(piece, piece, WS).then_inc(w_scaled, 1)
                gate(act, w_scaled, g + 1, act_past)
                copy(w[:, ds(j * (2 * WJ) + c * CH, CH)], piece).then_inc(w_hi, 1)

            def xn_normalise(b):
                gate(act, ln1, b * LN1_STEPS + LN1_STEPS, act_past)
                if isinstance(b, int) and b < 2:
                    wait(act, xn_lo, b)
                else:
                    gate(act, xn2_lo, b * 2 - 2, act_past)
                for i in range(NB):
                    ins = a.activation(xn32[:, i * D:(i + 1) * D], x1[:, ds(b * (NB * D) + i * D, D)],
                                       ACT.Identity, scale=rstd[0][:, i:i + 1], bias=nmr[:, i:i + 1])
                ins.then_inc(xn_put, 1)

            def xn_high(b):
                act.wait_ge(xn_put, b + 1)
                if isinstance(b, int) and b < 2:
                    wait(act, xnt_in, 16 * b)
                else:
                    gate(act, xn2t_in, 32 * b - 32, act_past)
                    act.wait_ge(xrow_in, 16 * b - 16)
                copy(xnrow[:, :].rearrange("p (n c) -> p n c", n=NB)[:, :, 0:D], blk(xn32[:, :])).then_inc(xn_hi, 1)

            xn_normalise(0)
            xn_high(0)
            act.wait_ge(qk_in, 48)
            act.wait_ge(small_in, 32)
            copy(wvs[:, 0:KD * D], tt[:, 0:1024].bitcast(F32), WS).then_inc(prep_hi, 1)
            copy(rw[:, 0:KD * E], tt[:, 1024:1024 + 2 * KD * E].bitcast(F32), WS).then_inc(prep_hi, 1)
            act.wait_ge(prep_mm, 1)
            copy(wm[:, 0:KD * D], PT0[:, :], WS).then_inc(prep_hi, 1)
            for c in range(2):
                w_split(c, c, 16, 0, c)

            def ffn_half(t, half, inline=False):
                tanh(t, half, inline)
                split_h(t, half, inline)

            def tanh(t, half, inline=False):
                act.wait_ge(gu_mm, t * 2 + half + 1)
                if not inline:
                    act.wait_ge(f_lo, t * 2 - 2 + half + 1)
                a.activation(th[:, half * 512:(half + 1) * 512], G[half][:, :], ACT.Tanh,
                             scale=0.5 / WS).then_inc(f_tanh, 1)

            def split_h(t, half, inline=False):
                act.wait_ge(f_h, t * 2 + half + 1)
                if not inline:
                    act.wait_ge(dn_mm, t * 2 - 2 + half + 1)
                copy(h[:, half * 512:(half + 1) * 512], th[:, half * 512:(half + 1) * 512]).then_inc(f_hi, 1)

            def xn2_high(b, par, h2):
                if h2 == 0:
                    act.wait_ge(xnt_in, 16 * B if isinstance(b, int) and b == B - 1 else 16 * b + 32)
                act.wait_ge(xn2_put, NB * b + 2 * h2 + 2)
                copy(xnrow[:, :].rearrange("p (n c) -> p n c", n=NB)[:, 2 * h2:2 * h2 + 2, 0:D],
                     blk(xn32[:, :])[:, 2 * h2:2 * h2 + 2]).then_inc(xn2_hi, 1)

            def t_high(b, first=False):
                for m in range(KD):
                    act.wait_ge(t_mm, b * KD + (m + 1))
                    if first:
                        act.wait_ge(prep_lo, 3)
                    wait(act, s_mm, b * NB)
                    copy(tt[:, m * S:(m + 1) * S], T_BANK[m][:, :]).then_inc(t_hi, 1)

            def batch(b, par, first=False, final=False):
                for m in range(2):
                    act.wait_ge(v_mm, 2 * b + m + 1)
                    wait(act, pv_mm, 2 * b)
                    copy(v[:, m * S:(m + 1) * S], V_BANK[m][:, :]).then_inc(v_hi, 1)
                if first:
                    xn_normalise(1)
                    xn_high(1)
                else:
                    w_split(b * CHUNKS + 2, 0, 32 * b + 32, b, 2)
                    w_split(b * CHUNKS + 3, 1, 32 * b + 32, b, 3)
                for q in range(NB):
                    n = (q + 1) * P
                    sbank = S_BANK[q]
                    act.wait_ge(s_nm, NB * b + q + 1)
                    if q == 0:
                        wait(act, x1_put, NB * b)
                        if first:
                            act.wait_ge(dump_in, 16)
                    if q == 3:
                        if not first:
                            tanh(2 * b - 2, 0, inline=True)
                        act.wait_ge(p_lo, NB * b + 2)
                    a.activation(p32[:, P32_AT[q]:P32_AT[q] + n], sbank[:, 0:n], ACT.Exp,
                                 bias=nm[:, q:q + 1], scale=1.0 / (16.0 * WS),
                                 accum_out=sums[:, q:q + 1]).then_inc(s_exp, 1)
                    if q == NB - 1 and not first:
                        act.wait_ge(lg_read, b)
                        a.activation(ez[:, :], z[:, :], ACT.Exp, scale=-1.0).then_inc(r_exp, 1)
                    act.wait_ge(s_exp, NB * b + q + 1)
                    if q == 3:
                        act.wait_ge(pt_in[1], 16 * b + 16)
                    else:
                        wait(act, pt_in[3 if q == 1 else q], 16 * b)
                    copy(phl[:, PHL_AT[q]:PHL_AT[q] + n], p32[:, P32_AT[q]:P32_AT[q] + n]).then_inc(p_hi, 1)
                if not first:
                    tanh(2 * b - 2, 1, inline=True)
                    split_h(2 * b - 2, 0, inline=True)
                if not first and not final:
                    xn_normalise(b + 1)
                if not first:
                    split_h(2 * b - 2, 1, inline=True)
                    tanh(2 * b - 1, 0)
                if not first and not final:
                    xn_high(b + 1)
                if not first and not final:
                    tanh(2 * b - 1, 1)
                if first:
                    w_split(2, 0, 32, 0, 2)
                    w_split(3, 1, 32, 0, 3)
                w_split(b * CHUNKS + CHUNKS, 0, 32 * b + 48, b + 1, 0)
                w_split(b * CHUNKS + (CHUNKS + 1), 1, 32 * b + 48, b + 1, 1)
                if final:
                    tanh(2 * b - 1, 1)
                if not first:
                    split_h(2 * b - 1, 0)
                if not first and not final:
                    split_h(2 * b - 1, 1)
                if not final:
                    t_high(b + 1)
                for h2 in range(2):
                    xn2_high(b, par, h2)
                if final:
                    split_h(2 * b - 1, 1)

            t_high(0, first=True)
            batch(0, 0, first=True)
            with act.Fori(1, B - 2, 2) as b:
                for s in range(2):
                    batch(b + s, (1 + s) % 2)
            batch(B - 1, (B - 1) % 2, final=True)
            for c in (2, 3):
                w_split(E * CHUNKS + c, c % 2, 32 * E + 32, E, c)
            act.wait_ge(lg_read, B)
            a.activation(ez[:, :], z[:, :], ACT.Exp, scale=-1.0).then_inc(r_exp, 1)
            for t in (SHARED - 2, SHARED - 1):
                for half in range(2):
                    ffn_half(t, half)

            def y_copy(n, slot, cnt, free):
                j = act.value_load(w_tab[0:1, ds(n, 1)], min_val=0, max_val=E)
                gate(act, ax_in[slot], cnt, act_past)
                gate(act, y_out, free, act_past)
                gate(act, dn_mm, n * 2 + (2 * SHARED + 2), act_past)
                for c in range(2):
                    ins = a.activation(ysb[:, (slot * 2 + c) * D:(slot * 2 + c + 1) * D], Y[:, c * D:(c + 1) * D],
                                       ACT.Copy, scale=aux[:, :].bitcast(F32)[
                                           :, ds(j + (slot * AW + c * (1 + E)), 1)])
                ins.then_inc(y_read, 1)

            def tile(n, before=None):
                ffn_half(n + SHARED, 0)
                if before is not None:
                    y_copy(n - 1, *before)
                ffn_half(n + SHARED, 1)

            def block_h(b, slot):
                act.wait_ge(gu_mm, b + (2 * FFN0 + 1))
                act.wait_ge(f_lo, b + (2 * FFN0 - 1))
                a.activation(th[:, slot * 512:(slot + 1) * 512], G[slot][:, :], ACT.Tanh,
                             scale=0.5 / WS).then_inc(f_tanh, 1)
                act.wait_ge(f_h, b + (2 * FFN0 + 1))
                if isinstance(b, int) and b < 2:
                    act.wait_ge(dn_mm, 2 * FFN0)
                else:
                    act.wait_ge(ht_in[slot], b * 8 - 8 * slot)
                copy(h[:, slot * 1024:slot * 1024 + 512], th[:, slot * 512:(slot + 1) * 512]).then_inc(f_hi, 1)

            def y_copy_block(b, slot):
                j = act.value_load(w_tab[0:1, ds(b + PAIRS, 1)], min_val=0, max_val=E)
                if isinstance(b, int) and b == 0:
                    gate(act, y_out, 32 * (PAIRS - 1), act_past)
                else:
                    gate(act, y_out, b * 16 + (32 * PAIRS - 16), act_past)
                gate(act, dn_mm, b + (2 * FFN0 + 1), act_past)
                a.activation(ysb[:, slot * 2 * D:(slot * 2 + 1) * D], YB[slot][:, 0:D], ACT.Copy,
                             scale=aux_b[:, ds(j + b * (1 + E), 1)]).then_inc(y_read, 1)

            act.wait_ge(tab, T_STEPS)
            tile(0)
            tile(1, (0, 16, 0))
            tile(2, (1, 16, 0))
            with act.Fori(3, PAIRS - 1, 2) as n:
                for s in range(2):
                    tile(n + s, (s, n * 8 + 8, n * 32 - (64 - 32 * s)))
            n = PAIRS - 1
            tile(n, ((n - 1) % 2, 16 * ((n - 1) // 2 + 1), 32 * (n - 2)))
            act.wait_ge(tab2, T2_STEPS)
            block_h(0, 0)
            y_copy(n, 1, 8 * PAIRS, 32 * (n - 1))
            block_h(1, 1)
            act.wait_ge(aux_b_in, 16 * SINGLES)
            block_h(2, 0)
            y_copy_block(0, 0)
            with act.Fori(3, SINGLES, 2) as b:
                for s in range(2):
                    block_h(b + s, 1 - s)
                    y_copy_block(b + (s - 2), 1 - s)
            for b in range(SINGLES - 2, SINGLES):
                y_copy_block(b, b % 2)

        @block.vector
        def _(dve):
            d = nc.vector
            d.memset(xrow[0][:, 0:2 * RW], 0.0).then_inc(c_dve, 1)
            d.memset(p32[:, 0:2 * D], 0.0).then_inc(c_dve, 1)
            d.memset(cum[:, :], 0.0).then_inc(c_dve, 1)
            d.memset(cumh[:, :], 0.0).then_inc(c_dve, 1)

            def low(o, full, hi, scale=None):
                if scale is None:
                    return d.tensor_tensor(o, full, hi, ALU.subtract)
                return d.scalar_tensor_tensor(out=o, in0=full, scalar=scale, in1=hi, op0=ALU.mult, op1=ALU.subtract)

            def stats_of(i, lns, steps, run, src, between=None):
                c = Chain(dve, lns, steps, run)
                for n in range(NB):
                    ins = d.bn_stats(stats[:, 6 * n:6 * n + 6], src(n))
                c.then(ins)
                if between is not None:
                    between()
                aggregate(i, c)
                return c

            def aggregate(i, c):
                gate(dve, c.sem, c.run * c.per + 1, dve_past)
                for n in range(NB):
                    c.then(d.bn_aggr(mv[i][:, 2 * n:2 * n + 2], stats[:, 6 * n:6 * n + 6]))
                c.last()
                c.then(d.tensor_scalar(ve[i][:, :], mv[i][:, :].rearrange("p (n c) -> p n c", c=2)[:, :, 1],
                                       EPS, None, ALU.add))

            def shift_of(run, c):
                dve.wait_ge(rstd1_rdy, run + 1)
                c.then(d.scalar_tensor_tensor(out=nmr[:, :], in0=mv[0][:, :].rearrange("p (n c) -> p n c", c=2)[:, :, 0],
                                              scalar=-1.0, in1=rstd[0][:, :], op0=ALU.mult, op1=ALU.mult))

            def x_of(b):
                return lambda i: x1[:, ds(b * (NB * D) + i * D, D)]

            dve.wait_ge(x_first, 16)
            shift_of(0, stats_of(0, ln1, LN1_STEPS, 0, x_of(0)))
            dve.wait_ge(xn_hi, 1)
            xn0 = xnrow[:, :].rearrange("p (n c) -> p n c", n=NB)
            low(xn0[:, :, D:2 * D], blk(xn32[:, :]), xn0[:, :, 0:D]).then_inc(xn_lo, 1)
            dve.wait_ge(prep_hi, 2)
            low(wvs[:, KD * D:2 * KD * D], tt[:, 0:1024].bitcast(F32), wvs[:, 0:KD * D], WS).then_inc(prep_lo, 1)
            low(rw[:, KD * E:2 * KD * E], tt[:, 1024:1024 + 2 * KD * E].bitcast(F32), rw[:, 0:KD * E],
                WS).then_inc(prep_lo, 1)
            dve.wait_ge(prep_hi, 3)
            low(wm[:, KD * D:2 * KD * D], PT0[:, :], wm[:, 0:KD * D], WS).then_inc(prep_lo, 1)
            dve.wait_ge(small_in, 32)
            for i in range(1, NB):
                ins = d.tensor_copy(biases[:, i * E:(i + 1) * E], biases[:, 0:E])
            ins.then_inc(prep_lo, 1)
            dve.wait_ge(x_second, 16)
            c1 = stats_of(0, ln1, LN1_STEPS, 1, x_of(1))
            dve.wait_ge(xn_put, 1)
            shift_of(1, c1)
            dve.wait_ge(c_rdy, 1)

            b3 = lambda t_: t_[:, :].rearrange("p (n e) -> p n e", e=E)

            def read_logits(r, o=Y):
                dve.wait_ge(lg_mm, r + 1)
                d.scalar_tensor_tensor(out=z[:, :], in0=o[:, 0:NB * E], scalar=1.0 / WS, in1=biases[:, :],
                                       op0=ALU.mult, op1=ALU.add).then_inc(lg_read, 1)

            def route(r):
                c = Chain(dve, r_dve, R_STEPS, r)
                dve.wait_ge(r_exp, r + 1)
                c.then(d.tensor_scalar(pr2[:, :], ez[:, :], 1.0, None, ALU.add)); c.last()
                c.then(d.reciprocal(pr[:, :], pr2[:, :]))
                gate(dve, r_dve, r * R_STEPS + c.k, dve_past)
                for n in range(NB):
                    ins = d.max(mx8[:, n * E:(n + 1) * E], pr[:, n * E:(n + 1) * E])
                c.then(ins)
                gate(dve, r_dve, r * R_STEPS + c.k, dve_past)
                for n in range(NB):
                    ins = d.max_index(ix8[:, n * E:(n + 1) * E], mx8[:, n * E:(n + 1) * E], pr[:, n * E:(n + 1) * E])
                c.then(ins); c.last()
                return c

            def one_hots(r, c):
                c.then(d.tensor_copy(idxf[:, :].rearrange("p (k n) -> p k n", k=TOPK),
                                     ix8[:, :].rearrange("p (n e) -> p e n", e=E)[:, 0:TOPK, :])); c.last()
                c.then(d.tensor_tensor(b3(one_hot), eidx[:, :].unsqueeze(1).to_broadcast([P, TOPK * NB, E]),
                                       idxf[:, :].unsqueeze(2).to_broadcast([P, TOPK * NB, E]), ALU.is_equal)); c.last()
                c.then(d.tensor_tensor(mask[:, :], one_hot[:, 0:NB * E], one_hot[:, NB * E:2 * NB * E], ALU.add))
                assert c.k == R_MASK

            def weights(r, par, c):
                mxk = mx8[:, :].rearrange("p (n e) -> p e n", e=E)
                c.last()
                c.then(d.tensor_tensor(den[:, :], mxk[:, 0, :], mxk[:, 1, :], ALU.add))
                c.then(d.tensor_tensor(wv_[:, :], pr[:, :], mask[:, :], ALU.mult)); c.last()
                c.then(d.reciprocal(rden[:, :], den[:, :]))
                c.then(d.tensor_reduce(msum[:, :], mask[:, :].rearrange("p (n e) -> p e n", n=NB), X, ALU.add)); c.last()
                if par == 0:
                    dve.wait_ge(rows_in, ZERO_ROWS)
                c.then(d.scalar_tensor_tensor(
                    out=xrow[par][:, :].bitcast(F32).rearrange("p (n c) -> p n c", n=NB)[:, :, D + 1:RC],
                    in0=b3(wv_), scalar=1.0 / WS, in1=rden[:, :].unsqueeze(2).to_broadcast([P, NB, E]),
                    op0=ALU.mult, op1=ALU.mult))
                c.then(d.tensor_tensor(cum[:, :], cum[:, :], msum[:, :], ALU.add)); c.last()
                assert c.k == c.per, c.k

            def places(r):
                dve.wait_ge(px_mm, r + 1)
                d.tensor_tensor(pos[:, :], PX_BANK[:, 0:NB * E], base[:, :], ALU.add).then_inc(px_dve, 1)
                d.tensor_copy(cumh[:, :], cum[:, :]).then_inc(px_dve, 1)

            def row_numbers(r):
                dve.wait_ge(px_dve, r * 3 + 2)
                d.tensor_tensor(pm[:, :].rearrange("p (k m) -> p k m", k=TOPK),
                                pos[:, :].unsqueeze(1).to_broadcast([P, TOPK, NB * E]),
                                one_hot[:, :].rearrange("p (k m) -> p k m", k=TOPK), ALU.mult).then_inc(px_dve, 1)
                dve.wait_ge(px_dve, r * 3 + 3)
                if not (isinstance(r, int) and r == B - 1):
                    dve.wait_ge(rows_in, ROWS_PER * r + ZERO_ROWS)
                d.tensor_reduce(sidx_of(r), b3(pm), X, ALU.add).then_inc(sidx_rdy, 1)

            def ffn_half(t, half):
                h_of(t * 2 + half + 1, half)

            def h_of(count, half):
                g, u = G[half], U[half]
                tb = th[:, half * 512:(half + 1) * 512]
                dve.wait_ge(f_tanh, count)
                d.scalar_tensor_tensor(out=tb, in0=tb, scalar=1.0, in1=g[:, :], op0=ALU.add,
                                       op1=ALU.mult).then_inc(f_sg, 1)
                dve.wait_ge(f_sg, count)
                d.scalar_tensor_tensor(out=tb, in0=tb, scalar=0.5 / (WS * WS), in1=u[:, :], op0=ALU.mult,
                                       op1=ALU.mult).then_inc(f_h, 1)
                return tb

            def ffn_low(t, half):
                tb = th[:, half * 512:(half + 1) * 512]
                dve.wait_ge(f_hi, t * 2 + half + 1)
                low(h[:, (2 + half) * 512:(3 + half) * 512], tb, h[:, half * 512:(half + 1) * 512]).then_inc(f_lo, 1)

            def add_shared(t, blk0, y=Y):
                dve.wait_ge(dn_mm, t * 2 + 2)
                o = x1[:, ds(blk0 * D, 2 * D)]
                d.scalar_tensor_tensor(out=o, in0=y[:, :], scalar=1.0 / WS, in1=o, op0=ALU.mult,
                                       op1=ALU.add).then_inc(y_read, 1)

            def ln2_put(b, h2):
                if h2 == 0:
                    dve.wait_ge(xn_lo, b + 2 if not isinstance(b, int) or b < B - 1 else B)
                    dve.wait_ge(rstd2_rdy, b + 1)
                for i in (2 * h2, 2 * h2 + 1):
                    d.tensor_scalar(xn32[:, i * D:(i + 1) * D], x_of(b)(i), mv[1][:, 2 * i:2 * i + 1],
                                    rstd[1][:, i:i + 1], ALU.subtract, ALU.mult).then_inc(xn2_put, 1)

            def ln2_low(b, par, h2):
                dve.wait_ge(xn2_hi, 2 * b + h2 + 1)
                r0 = xnrow[:, :].rearrange("p (n c) -> p n c", n=NB)[:, 2 * h2:2 * h2 + 2]
                low(r0[:, :, D:2 * D], blk(xn32[:, :])[:, 2 * h2:2 * h2 + 2], r0[:, :, 0:D]).then_inc(xn2_lo, 1)

            def t_low(b, m):
                dve.wait_ge(t_hi, b * KD + (m + 1))
                low(tt[:, (KD + m) * S:(KD + m + 1) * S], T_BANK[m][:, :],
                    tt[:, m * S:(m + 1) * S]).then_inc(t_lo, 1)

            def batch(b, par, first=False, final=False):
                for m in range(2):
                    dve.wait_ge(v_hi, 2 * b + m + 1)
                    low(v[:, (2 + m) * S:(3 + m) * S], V_BANK[m][:, :],
                        v[:, m * S:(m + 1) * S]).then_inc(v_lo, 1)
                if not first and not final:
                    c1 = stats_of(0, ln1, LN1_STEPS, b + 1, x_of(b + 1))

                def p_low(q):
                    n = (q + 1) * P
                    dve.wait_ge(p_hi, NB * b + q + 1)
                    low(phl[:, PHL_AT[q] + n:PHL_AT[q] + 2 * n], p32[:, P32_AT[q]:P32_AT[q] + n],
                        phl[:, PHL_AT[q]:PHL_AT[q] + n]).then_inc(p_lo, 1)

                for q in range(NB):
                    n = (q + 1) * P
                    dve.wait_ge(s_mm, NB * b + q + 1)
                    if q == 0:
                        wait(dve, s_exp, NB * b)
                    d.tensor_reduce(mx[:, q:q + 1], S_BANK[q][:, 0:n], X, ALU.max).then_inc(s_max, 1)
                    dve.wait_ge(s_max, NB * b + q + 1)
                    d.tensor_scalar(nm[:, q:q + 1], mx[:, q:q + 1], -1.0 / (16.0 * WS), None,
                                    ALU.mult).then_inc(s_nm, 1)
                    if q:
                        p_low(q - 1)
                if not first:
                    read_logits(b - 1)
                    ta, tb = 2 * b - 2, 2 * b - 1
                    ffn_half(ta, 0)
                p_low(NB - 1)
                if not first and not final:
                    shift_of(b + 1, c1)
                if not first:
                    ffn_half(ta, 1)
                    ffn_low(ta, 0)
                    chain = route(b - 1)
                    one_hots(b - 1, chain)
                    ffn_low(ta, 1)
                    ffn_half(tb, 0)
                dve.wait_ge(s_exp, NB * b + NB)
                d.tensor_scalar(s16[:, :], sums[:, :], WS, None, ALU.mult).then_inc(sum_dve, 1)
                dve.wait_ge(sum_dve, 2 * b + 1)
                d.reciprocal(rs[:, :], s16[:, :]).then_inc(sum_dve, 1)
                def place_rows():
                    weights(b - 1, 1 - par, chain)
                    places(b - 1)

                if not first and not final:
                    ffn_half(tb, 1)
                    place_rows()
                dve.wait_ge(sum_dve, 2 * b + 2)
                for h2 in range(2):
                    dve.wait_ge(pv_mm, 2 * b + h2 + 1)
                    for q in (2 * h2, 2 * h2 + 1):
                        o = x1[:, ds(b * (NB * D) + q * D, D)]
                        d.scalar_tensor_tensor(out=o, in0=PV_BANK[h2][:, (q % 2) * D:(q % 2 + 1) * D],
                                               scalar=rs[:, q:q + 1], in1=o, op0=ALU.mult,
                                               op1=ALU.add).then_inc(x1_put, 1)
                if not first and not final:
                    ffn_low(tb, 0)
                gate(dve, x1_put, NB * b + NB, dve_past)
                stats_of(1, ln2, LN2_STEPS, b, x_of(b),
                         None if first or final else lambda: ffn_low(tb, 1))
                if final:
                    place_rows()
                if not first:
                    row_numbers(b - 1)
                if not final:
                    t_low(b + 1, 0)
                for h2 in range(2):
                    ln2_put(b, h2)
                if not final:
                    t_low(b + 1, 1)
                if final:
                    ffn_low(tb, 0)
                    add_shared(ta, b * NB - NB)
                for h2 in range(2):
                    ln2_low(b, par, h2)
                if final:
                    ffn_half(tb, 1)
                    ffn_low(tb, 1)
                if not first and not final:
                    add_shared(ta, b * NB - NB)
                if not first:
                    add_shared(tb, b * NB - (NB - 2), YS_BANK[1])

            for m in range(KD):
                t_low(0, m)
            batch(0, 0, first=True)
            dve.wait_ge(x_early, 48)
            with dve.Fori(1, B - 2, 2) as b:
                for s in range(2):
                    if s == 1:
                        gate(dve, x_late, b * 8 + 8, dve_past)
                    batch(b + s, (1 + s) % 2)
            batch(B - 1, (B - 1) % 2, final=True)
            read_logits(B - 1, PT0)
            chain = route(B - 1)
            one_hots(B - 1, chain)
            weights(B - 1, (B - 1) % 2, chain)
            places(B - 1)
            row_numbers(B - 1)
            for half in range(2):
                ffn_half(SHARED - 2, half)
                ffn_low(SHARED - 2, half)

            r_ = lambda i: tf[0:1, i * E:(i + 1) * E]
            CF, INC, PREV, VAL, TMP, ONE, STEP, NBL, BASE, USED = (r_(i) for i in range(10))
            CNT = PT2[0:1, 0:E]

            def table(c, n, first, unit):
                t3 = lambda t_: t_[0:1, 0:n * E].rearrange("p (t e) -> p t e", e=E)
                per_piece = lambda t_: t_.unsqueeze(1).to_broadcast([1, n, E])
                t1 = lambda i: tsum[0:1, i * PAIRS:i * PAIRS + n]
                c.then(d.tensor_tensor_scan(INC, ONE, CF, 0.0, ALU.mult, ALU.add)); c.last()
                c.then(d.tensor_tensor(PREV, INC, CF, ALU.subtract))
                c.then(d.tensor_tensor(t3(oh), t3(tio), per_piece(INC), ALU.is_ge)); c.last()
                c.then(d.scalar_tensor_tensor(out=VAL, in0=PREV, scalar=float(unit), in1=BASE, op0=ALU.mult,
                                              op1=ALU.add))
                c.then(d.tensor_reduce(t1(1), t3(oh), X, ALU.add)); c.last()
                c.then(d.tensor_tensor(STEP[:, 0:E - 1], VAL[:, 1:E], VAL[:, 0:E - 1], ALU.subtract))
                c.then(d.tensor_scalar(w_tab[0:1, first:first + n], t1(1), 1.0, float(E), ALU.add, ALU.min)); c.last()
                c.then(d.tensor_tensor(t3(ot), t3(oh), per_piece(STEP), ALU.mult)); c.last()
                c.then(d.tensor_reduce(t1(0), t3(ot), X, ALU.add)); c.last()
                c.then(d.scalar_tensor_tensor(out=t1(1), in0=t1(0), scalar=VAL[:, 0:1],
                                              in1=tneg[0:1, first:first + n], op0=ALU.add, op1=ALU.add)); c.last()
                c.then(d.tensor_scalar(start_tab[0:1, first:first + n], t1(1), float(SPARE), None, ALU.min))
                assert c.k == c.per, c.k

            c = Chain(dve, tab, T_STEPS, 0)
            dve.wait_ge(tio_rdy, 1)
            c.then(d.memset(ONE, 1.0))
            c.then(d.memset(STEP, FAR))
            dve.wait_ge(cnt_mm, 1)
            c.then(d.tensor_scalar(ti[0:1, 0:E], CNT, float(P - 1), None, ALU.add)); c.last()
            c.then(d.tensor_single_scalar(ti[0:1, E:2 * E], ti[0:1, 0:E], TT.bit_length() - 1,
                                          ALU.logical_shift_right))
            c.then(d.tensor_single_scalar(ti[0:1, 0:E], ti[0:1, 0:E], P.bit_length() - 1,
                                          ALU.logical_shift_right)); c.last()
            c.then(d.tensor_copy(CF, ti[0:1, E:2 * E]))
            c.then(d.tensor_copy(NBL, ti[0:1, 0:E]))
            c.then(d.scalar_tensor_tensor(out=BASE, in0=CNT, scalar=-float(TT), in1=base[0:1, 0:E],
                                          op0=ALU.add, op1=ALU.add)); c.last()
            table(c, PAIRS, 0, TT)

            def table_of_singles():
                c = Chain(dve, tab2, T2_STEPS, 0)
                dve.wait_ge(tab, T_STEPS)
                c.then(d.tensor_scalar(USED, PREV, -1.0, float(PAIRS), ALU.mult, ALU.add)); c.last()
                c.then(d.scalar_tensor_tensor(out=USED, in0=USED, scalar=0.0, in1=CF, op0=ALU.max,
                                              op1=ALU.min)); c.last()
                c.then(d.scalar_tensor_tensor(out=CF, in0=USED, scalar=-2.0, in1=NBL, op0=ALU.mult, op1=ALU.add))
                c.then(d.scalar_tensor_tensor(out=TMP, in0=USED, scalar=-float(TT), in1=BASE, op0=ALU.mult,
                                              op1=ALU.add)); c.last()
                c.then(d.tensor_scalar(BASE, TMP, float(TT - P), None, ALU.add)); c.last()
                table(c, SINGLES, PAIRS, P)

            ffn_half(SHARED - 1, 0)
            add_shared(SHARED - 2, T // P - 4)
            ffn_low(SHARED - 1, 0)
            ffn_half(SHARED - 1, 1)
            ffn_low(SHARED - 1, 1)
            table_of_singles()

            def tile(n, shared_before=False):
                t = n + SHARED
                ffn_half(t, 0)
                if shared_before:
                    add_shared(SHARED - 1, T // P - 2)
                ffn_low(t, 0)
                ffn_half(t, 1)
                ffn_low(t, 1)

            tile(0, True)
            with dve.Fori(1, PAIRS) as n:
                tile(n)

            def block_h(b, slot):
                i = b + (2 * FFN0 + 1)
                tb = h_of(i, slot)
                dve.wait_ge(f_hi, i)
                low(h[:, slot * 1024 + 512:(slot + 1) * 1024], tb,
                    h[:, slot * 1024:slot * 1024 + 512]).then_inc(f_lo, 1)

            with dve.Fori(0, SINGLES - 1, 2) as b:
                for s in range(2):
                    block_h(b + s, s)
            block_h(SINGLES - 1, 0)

        @block.tensor
        def _(pe):
            mm = nc.tensor.matmul

            pe.wait_ge(qk_in, 48)
            for m in range(KD):
                for k in range(KD):
                    ins = mm(PT0[:, m * D:(m + 1) * D], v[:, 0:1024].bitcast(F32)[:, k * D + m * P:k * D + (m + 1) * P],
                             v[:, 1024:2048].bitcast(F32)[:, k * D:(k + 1) * D], start=(k == 0), stop=(k == KD - 1))
            ins.then_inc(prep_mm, 1)
            pe.wait_ge(prep_lo, 4)
            pe.wait_ge(c_rdy, 1)

            xn4 = xnt[:, :].rearrange("p (n c r) -> p n c r", n=NB, r=P)
            xn24 = xn2t[:, :].rearrange("p (n c r) -> p n c r", n=NB, r=P)

            def gate_up(t, half, j, moving, shape3, covered=False):
                if not covered:
                    pe.wait_ge(f_h, t * 2 - 2 + half + 1)
                for m, o in enumerate((G[half], U[half])):
                    for i in range(2):
                        dst = o[:, i * TT:(i + 1) * TT]
                        if shape3:
                            dst = dst.rearrange("p (n r) -> p n r", r=P)
                        cnt = 0
                        for k in range(KD):
                            for ws, ms in PASSES:
                                ins = mm(dst, w_ap(j, ws, m * MAT + k * I + (2 * half + i) * P, P),
                                         moving(ms * KD + k), start=(cnt == 0), stop=(cnt == 3 * KD - 1))
                                cnt += 1
                ins.then_inc(gu_mm, 1)

            def down(t, j, covered=False, o=Y):
                if not covered:
                    pe.wait_ge(y_read, t)
                cnt = 0
                for half in range(2):
                    pe.wait_ge(f_lo, t * 2 + half + 1)
                    for i in (2 * half, 2 * half + 1):
                        for hs, ws in PASSES:
                            for a in range(2):
                                ins = mm(o[:, a * D:(a + 1) * D],
                                         h[:, (hs * KI + i) * TT + a * P:(hs * KI + i) * TT + (a + 1) * P],
                                         w_ap(j, ws, 2 * MAT + i * D, D), start=(cnt == 0),
                                         stop=(cnt == 6 * KI - 1), skip_group_check=True)
                                cnt += 1
                    ins.then_inc(dn_mm, 1)

            def logits(r, last=False):
                pe.wait_ge(xn2t_in, r * 32 + 32)
                src, o = (xn4, PT0) if last else (xn24, Y)
                for i in range(NB):
                    cnt = 0
                    for k in range(KD):
                        for xs, ws in PASSES:
                            ins = mm(o[:, i * E:(i + 1) * E], src[:, i, xs * KD + k, :],
                                     rw[:, (ws * KD + k) * E:(ws * KD + k + 1) * E],
                                     start=(cnt == 0), stop=(cnt == 3 * KD - 1))
                            cnt += 1
                ins.then_inc(lg_mm, 1)

            def prefix(r):
                pe.wait_ge(r_dve, r * R_STEPS + R_MASK)
                mm(PX_BANK[:, 0:NB * E], tri[:, :], mask[:, :], start=True, stop=False)
                for i in range(NB - 1):
                    n = NB - 1 - i
                    mm(PX_BANK[:, (i + 1) * E:NB * E].rearrange("p (n e) -> p n e", e=E), ones[:, :],
                       mask[:, i * E:(i + 1) * E].unsqueeze(1).to_broadcast([P, n, E]),
                       start=False, stop=False)
                mm(PX_BANK[:, 0:NB * E].rearrange("p (n e) -> p n e", e=E), ones[:, :],
                   cumh[:, :].unsqueeze(1).to_broadcast([P, NB, E]), start=False, stop=True).then_inc(px_mm, 1)

            def pv(b):
                off = 0
                for q in range(NB):
                    pe.wait_ge(pt_in[q], b * 16 + 16)
                    cnt, total = 0, 3 * (q + 1)
                    for kb in range(q + 1):
                        for ps, vs in PASSES:
                            ins = mm(PV_BANK[q // 2][:, (q % 2) * D:(q % 2 + 1) * D],
                                     ptr[:, off + (ps * (q + 1) + kb) * P:off + (ps * (q + 1) + kb + 1) * P],
                                     v[:, (vs * NB + kb) * D:(vs * NB + kb + 1) * D],
                                     start=(cnt == 0), stop=(cnt == total - 1))
                            cnt += 1
                    off += 2 * (q + 1) * P
                    if q % 2:
                        ins.then_inc(pv_mm, 1)

            def half_batch(src4, i):
                return lambda c: src4[:, 2 * i:2 * i + 2, c, :]

            def t_product(b):
                pe.wait_ge(xnt_in, b * 16 + 16)
                wait(pe, x1_put, b * NB - 2)
                for m in range(KD):
                    cnt = 0
                    for k in range(KD):
                        for ws, ms in PASSES:
                            ins = mm(T_BANK[m][:, :].rearrange("p (n r) -> p n r", r=P),
                                     wm[:, (ws * KD + k) * D + m * P:(ws * KD + k) * D + (m + 1) * P],
                                     xn4[:, :, ms * KD + k, :], start=(cnt == 0), stop=(cnt == 3 * KD - 1))
                            cnt += 1
                    ins.then_inc(t_mm, 1)

            def batch(b, first=False, final=False):
                for m in range(2):
                    if m == 0:
                        wait(pe, x1_put, NB * b)
                    for i in range(2):
                        cnt = 0
                        for k in range(KD):
                            for xs, ws in PASSES:
                                ins = mm(V_BANK[m][:, i * D:(i + 1) * D], xn4[:, 2 * m + i, xs * KD + k, :],
                                         wvs[:, (ws * KD + k) * D:(ws * KD + k + 1) * D],
                                         start=(cnt == 0), stop=(cnt == 3 * KD - 1))
                                cnt += 1
                    ins.then_inc(v_mm, 1)
                for q in range(NB):
                    o = S_BANK[q]
                    if q == 0:
                        pe.wait_ge(t_lo, KD * b + 2)
                    elif q == 3:
                        pe.wait_ge(v_lo, 2 * b + 1)
                    n = q + 1
                    cnt = 0
                    for k in range(KD):
                        for ts, ms in PASSES:
                            lhs = tt[:, (ts * KD + k) * S + q * P:(ts * KD + k) * S + (q + 1) * P]
                            mm(o[:, 0:n * P].rearrange("p (n r) -> p n r", r=P), lhs,
                               xn4[:, 0:n, ms * KD + k, :], start=(cnt == 0), stop=(cnt == 3 * KD - 1))
                            cnt += 1
                    mm(o[:, q * P:n * P], ident[:, :], maskb[:, :], start=False, stop=True,
                       skip_group_check=True).then_inc(s_mm, 1)
                if not first:
                    logits(b - 1)
                    pe.wait_ge(w_lo, CHUNKS)
                    ta, tb = 2 * b - 2, 2 * b - 1
                    gate_up(ta, 0, 0, half_batch(xn24, 0), True, covered=True)
                    pe.wait_ge(v_lo, 2 * b + 2)
                    pe.wait_ge(s_exp, NB * b + 1)
                    gate_up(ta, 1, 0, half_batch(xn24, 0), True, covered=True)
                    gate_up(tb, 0, 0, half_batch(xn24, 1), True)
                    pe.wait_ge(s_exp, NB * b + 2)
                    if not final:
                        gate_up(tb, 1, 0, half_batch(xn24, 1), True)
                        prefix(b - 1)
                pe.wait_ge(v_lo, 2 * b + 2)
                pe.wait_ge(s_exp, NB * b + 4)
                pv(b)
                if final:
                    gate_up(tb, 1, 0, half_batch(xn24, 1), True)
                    prefix(b - 1)
                if not first:
                    down(ta, 0, covered=True)
                if not final:
                    t_product(b + 1)
                if not first:
                    down(tb, 0, covered=True, o=YS_BANK[1])

            t_product(0)
            batch(0, first=True)
            with pe.Fori(1, B - 1) as b:
                batch(b)
            batch(B - 1, final=True)
            pe.wait_ge(px_dve, 3 * (B - 2) + 1)
            logits(B - 1, last=True)
            ta, tb = SHARED - 2, SHARED - 1
            pe.wait_ge(y_read, SHARED - 2)
            gate_up(ta, 0, 0, half_batch(xn4, 0), True)
            prefix(B - 1)
            gate_up(ta, 1, 0, half_batch(xn4, 0), True)
            pe.wait_ge(px_dve, 3 * B)
            mm(PT2[:, 0:E], ones[:, :], cumh[:, :], start=True, stop=True).then_inc(cnt_mm, 1)
            gate_up(tb, 0, 0, half_batch(xn4, 1), True)
            down(ta, 0)
            gate_up(tb, 1, 0, half_batch(xn4, 1), True)

            def expert(entry):
                return pe.value_load(w_tab[0:1, ds(entry, 1)], min_val=0, max_val=E)

            def block_gate_up(b, q, before):
                slot = q % 2
                j = expert(b + PAIRS)
                pe.wait_ge(xb_in[q], before * 16 + 16)
                pe.wait_ge(f_h, b + (2 * FFN0 - 1))
                for m, o in enumerate((G[slot], U[slot])):
                    cnt = 0
                    for k in range(KD):
                        for xs, ws in PASSES:
                            c = q * 4 + xs * KD + k
                            ins = mm(o[:, :], xt[:, c * P:(c + 1) * P], w_ap(j, ws, m * MAT + k * I, I),
                                     start=(cnt == 0), stop=(cnt == 3 * KD - 1))
                            cnt += 1
                ins.then_inc(gu_mm, 1)

            def block_down(b, slot):
                j = expert(b + PAIRS)
                pe.wait_ge(ht_in[slot], b * 8 + (16 - 8 * slot))
                pe.wait_ge(y_read, FFN0 if isinstance(b, int) and b == 0 else b + (FFN0 - 1))
                cnt = 0
                for i in range(KI):
                    for hs, ws in PASSES:
                        c = slot * 8 + hs * KI + i
                        ins = mm(YB[slot][:, 0:D], ht[:, c * P:(c + 1) * P], w_ap(j, ws, 2 * MAT + i * D, D),
                                 start=(cnt == 0), stop=(cnt == 3 * KI - 1))
                        cnt += 1
                ins.then_inc(dn_mm, 1)

            def tile(n, slot, cnt, j, j_before, second=True):
                t = n + SHARED
                moving = lambda c: xt[:, (slot * 4 + c) * TT:(slot * 4 + c + 1) * TT]
                pe.wait_ge(xt_in[slot], cnt)
                gate_up(t, 0, j, moving, False)
                if second:
                    down(t - 1, expert(n - 1) if j_before is None else j_before)
                gate_up(t, 1, j, moving, False)

            down(tb, 0)
            pe.wait_ge(tab, T_STEPS)
            pe.wait_ge(w_lo, (E + 1) * CHUNKS)
            tile(0, 0, 16, expert(0), None, second=False)
            with pe.Fori(1, PAIRS - 1, 2) as n:
                j = expert(n)
                tile(n, 1, n * 8 + 8, j, None)
                j_next = expert(n + 1)
                tile(n + 1, 0, n * 8 + 24, j_next, j)
            tile(PAIRS - 1, 1, 8 * PAIRS, expert(PAIRS - 1), None)
            pe.wait_ge(tab2, T2_STEPS)
            block_gate_up(0, 0, 0)
            down(FFN0 - 1, expert(PAIRS - 1))
            block_gate_up(1, 1, 0)
            block_gate_up(2, 2, 0)
            block_down(0, 0)
            with pe.Fori(0, SINGLES // 4) as i:
                for s in range(4):
                    b = i * 4 + (3 + s)
                    block_gate_up(b, (3 + s) % 4, i if s == 0 else i + 1)
                    block_down(b - 2, (1 + s) % 2)
            for b in range(SINGLES - 2, SINGLES):
                block_down(b, b % 2)


def kernel(**inputs):
    import numpy as np
    import concourse.bacc as bacc
    from concourse.bass_utils import run_bass_kernel_spmd

    g = lambda n: np.asarray(inputs[n])
    nc = bacc.Bacc("TRN2", target_bir_lowering=False, num_devices=1)

    def up(a):
        return a.reshape(KD, P, I).transpose(1, 0, 2).reshape(P, KD * I)

    def down(a):
        return a.reshape(KI, P, D).transpose(1, 0, 2).reshape(P, KI * D)

    cols = [up(g("L0_ffn_shared_gate").T), up(g("L0_ffn_shared_up").T), down(g("L0_ffn_shared_down").T)]
    for e in range(E):
        cols += [up(g("L0_ffn_gate_w")[e]), up(g("L0_ffn_up_w")[e]), down(g("L0_ffn_down_w")[e])]
    arrays = {
        "x": np.ascontiguousarray(g("L0_attn_x").reshape(T, D)),
        "wq_t": np.ascontiguousarray(g("L0_attn_Wq").T),
        "wk_t": np.ascontiguousarray(g("L0_attn_Wk").T),
        "wv": np.ascontiguousarray(g("L0_attn_Wv")),
        "w_all": np.ascontiguousarray(np.concatenate(cols, axis=1)),
        "router": np.ascontiguousarray(g("L0_ffn_router_w").T),
        "bias": np.ascontiguousarray(g("L0_ffn_routing_bias")),
    }
    aps = {n: nc.dram_tensor(n, a.shape, F32, kind="ExternalInput").ap() for n, a in arrays.items()}
    out = nc.dram_tensor("out", (T + P, D), F32, kind="ExternalOutput").ap()
    build(nc, **aps, out=out)
    r = run_bass_kernel_spmd(nc, [arrays], core_ids=[0])
    return r.results[0]["out"][:T].reshape(B, S, D)
```
